# Optimizing a Trainium2 kernel written in Bass

```python
import numpy as np
import jax
import jax.numpy as jnp

def _softmax(x, axis=-1):
    return jax.nn.softmax(x, axis=axis)

def _gelu(x):
    return jax.nn.gelu(x, approximate=True)

def _silu(x):
    return jax.nn.silu(x)

def _sigmoid(x):
    return jax.nn.sigmoid(x)

def _layernorm(x, axis=-1, eps=1e-05):
    m = jnp.mean(x, axis=axis, keepdims=True)
    v = jnp.var(x, axis=axis, keepdims=True)
    return (x - m) / jnp.sqrt(v + eps)

def _scatter_add(tgt, idx, src, axis=0):
    return tgt.at[idx].add(src)

def _segment_sum(src, seg, n):
    return jax.ops.segment_sum(src, seg, n)
kernel_name = 'mk_xattn_ffn_d1_seqx_r4_acd5a2'

def setup_inputs(seed: int=0):
    np.random.seed(seed)
    _w = jnp.asarray

    def _rec_inputs():
        import jax
        import jax.numpy as jnp
        _rk = jax.random.key(seed)
        x = -0.0002928 + 1 * jax.random.normal(jax.random.fold_in(_rk, 1), (16, 256, 256), jnp.float32)
        _lenS = 256 - jax.random.randint(jax.random.fold_in(_rk, 7), (16,), 0, max(1, 256 // 4) + 1, jnp.int32)
        _lenS2 = 256 - jax.random.randint(jax.random.fold_in(_rk, 8), (16,), 0, max(1, 256 // 4) + 1, jnp.int32)
        _ctx_1024P = jax.random.normal(jax.random.fold_in(_rk, 11), (16, 16, 256), jnp.float32)
        _ctx_1024c = jax.random.dirichlet(jax.random.fold_in(_rk, 511), 0.3 * jnp.ones((16,), jnp.float32), (16, 256))
        _ctx_1024t = jnp.einsum('bsk,bkd->bsd', _ctx_1024c, _ctx_1024P)
        _ctx_1024t = _ctx_1024t * jax.lax.rsqrt(jnp.mean(jnp.square(_ctx_1024t)) + 1e-12) * 0.953939
        ctx_1024 = -1.39393e-06 + 0.999914 * (_ctx_1024t + 0.3 * jax.random.normal(jax.random.fold_in(_rk, 611), (16, 256, 256), jnp.float32))
        return (x, ctx_1024)
    x, ctx_1024 = _rec_inputs()

    def _L0_xattn_setup():
        import jax, jax.numpy as jnp
        import numpy as np
        import math
        EMBED_DIM = 256
        NUM_HEADS = 16
        HEAD_DIM = EMBED_DIM // NUM_HEADS
        BLOCK = 64
        SPARSITY = 0.05
        BATCH = 2
        SEQ = 512

        def _block_pattern(seq_len, block_size, sparsity_ratio, is_causal):
            nb = seq_len // block_size
            total = nb * nb
            keep = int(total * (1.0 - sparsity_ratio))
            idx = [(i, i) for i in range(nb)]
            band = max(1, int(math.sqrt(keep - nb) / 2))
            for i in range(nb):
                for o in range(1, band + 1):
                    if i + o < nb:
                        idx.append((i, i + o))
                        if not is_causal:
                            idx.append((i + o, i))
                    if not is_causal and i - o >= 0:
                        idx.append((i, i - o))
            for skip in (2, 4, 8, 16):
                if len(idx) >= keep:
                    break
                for i in range(0, nb - skip, skip):
                    if len(idx) < keep:
                        idx.append((i, i + skip))
                        if not is_causal and len(idx) < keep:
                            idx.append((i + skip, i))
            uniq = sorted(set(idx))
            if is_causal:
                uniq = [(r, c) for r, c in uniq if r >= c]
            uniq = uniq[:keep]
            rows = np.array([r for r, c in uniq], dtype=np.int32)
            cols = np.array([c for r, c in uniq], dtype=np.int32)
            return (rows, cols)
        ROWS, COLS = _block_pattern(SEQ, BLOCK, SPARSITY, is_causal=False)
        rng = jax.random.key(seed)
        ks = jax.random.split(rng, 7)
        wscale = EMBED_DIM ** (-0.5)
        return {'query': jax.random.normal(ks[0], (BATCH, SEQ, EMBED_DIM), jnp.float32), 'key': jax.random.normal(ks[1], (BATCH, SEQ, EMBED_DIM), jnp.float32), 'value': jax.random.normal(ks[2], (BATCH, SEQ, EMBED_DIM), jnp.float32), 'Wq': jax.random.normal(ks[3], (EMBED_DIM, EMBED_DIM), jnp.float32) * wscale, 'Wk': jax.random.normal(ks[4], (EMBED_DIM, EMBED_DIM), jnp.float32) * wscale, 'Wv': jax.random.normal(ks[5], (EMBED_DIM, EMBED_DIM), jnp.float32) * wscale, 'Wo': jax.random.normal(ks[6], (EMBED_DIM, EMBED_DIM), jnp.float32) * wscale}
    _L0_xattn_all = _L0_xattn_setup()
    _L0_xattn_in = {k: v for k, v in _L0_xattn_all.items() if k in ('Wq', 'Wk', 'Wv', 'Wo')}
    del _L0_xattn_all

    def _L0_ffn_setup():
        import jax, jax.numpy as jnp
        import numpy as np
        D_MODEL = 256
        HIDDEN = 1024
        N_ROUTING = 2
        key = jax.random.key(seed)
        ks = jax.random.split(key, 10)
        s = 0.02
        x = jax.random.normal(ks[0], (4, 1024, D_MODEL), dtype=jnp.float32)
        gate_w = jax.random.normal(ks[1], (N_ROUTING, D_MODEL), dtype=jnp.float32) * s
        w1 = jax.random.normal(ks[2], (N_ROUTING, D_MODEL, HIDDEN), dtype=jnp.float32) * s
        b1 = jax.random.normal(ks[3], (N_ROUTING, HIDDEN), dtype=jnp.float32) * s
        w2 = jax.random.normal(ks[4], (N_ROUTING, HIDDEN, D_MODEL), dtype=jnp.float32) * s
        b2 = jax.random.normal(ks[5], (N_ROUTING, D_MODEL), dtype=jnp.float32) * s
        sw1 = jax.random.normal(ks[6], (D_MODEL, HIDDEN), dtype=jnp.float32) * s
        sb1 = jax.random.normal(ks[7], (HIDDEN,), dtype=jnp.float32) * s
        sw2 = jax.random.normal(ks[8], (HIDDEN, D_MODEL), dtype=jnp.float32) * s
        sb2 = jax.random.normal(ks[9], (D_MODEL,), dtype=jnp.float32) * s
        return {'x': x, 'gate_w': gate_w, 'w1': w1, 'b1': b1, 'w2': w2, 'b2': b2, 'sw1': sw1, 'sb1': sb1, 'sw2': sw2, 'sb2': sb2}
    _L0_ffn_all = _L0_ffn_setup()
    _L0_ffn_in = {k: v for k, v in _L0_ffn_all.items() if k in ('gate_w', 'w1', 'b1', 'w2', 'b2', 'sw1', 'sb1', 'sw2', 'sb2')}
    del _L0_ffn_all
    return {'x': x, 'ctx_1024': ctx_1024, 'L0_xattn_Wq': _L0_xattn_in['Wq'], 'L0_xattn_Wk': _L0_xattn_in['Wk'], 'L0_xattn_Wv': _L0_xattn_in['Wv'], 'L0_xattn_Wo': _L0_xattn_in['Wo'], 'L0_ffn_gate_w': _L0_ffn_in['gate_w'], 'L0_ffn_w1': _L0_ffn_in['w1'], 'L0_ffn_b1': _L0_ffn_in['b1'], 'L0_ffn_w2': _L0_ffn_in['w2'], 'L0_ffn_b2': _L0_ffn_in['b2'], 'L0_ffn_sw1': _L0_ffn_in['sw1'], 'L0_ffn_sb1': _L0_ffn_in['sb1'], 'L0_ffn_sw2': _L0_ffn_in['sw2'], 'L0_ffn_sb2': _L0_ffn_in['sb2']}

def reference(x, ctx_1024, L0_xattn_Wq, L0_xattn_Wk, L0_xattn_Wv, L0_xattn_Wo, L0_ffn_gate_w, L0_ffn_w1, L0_ffn_b1, L0_ffn_w2, L0_ffn_b2, L0_ffn_sw1, L0_ffn_sb1, L0_ffn_sw2, L0_ffn_sb2):
    import jax
    import jax.numpy as jnp

    def _L0_xattn_ref(query, key, value, Wq, Wk, Wv, Wo):
        import jax, jax.numpy as jnp
        import numpy as np
        import math
        EMBED_DIM = 256
        NUM_HEADS = 16
        HEAD_DIM = EMBED_DIM // NUM_HEADS
        BLOCK = 64
        SPARSITY = 0.05
        BATCH = 2
        SEQ = 512

        def _block_pattern(seq_len, block_size, sparsity_ratio, is_causal):
            nb = seq_len // block_size
            total = nb * nb
            keep = int(total * (1.0 - sparsity_ratio))
            idx = [(i, i) for i in range(nb)]
            band = max(1, int(math.sqrt(keep - nb) / 2))
            for i in range(nb):
                for o in range(1, band + 1):
                    if i + o < nb:
                        idx.append((i, i + o))
                        if not is_causal:
                            idx.append((i + o, i))
                    if not is_causal and i - o >= 0:
                        idx.append((i, i - o))
            for skip in (2, 4, 8, 16):
                if len(idx) >= keep:
                    break
                for i in range(0, nb - skip, skip):
                    if len(idx) < keep:
                        idx.append((i, i + skip))
                        if not is_causal and len(idx) < keep:
                            idx.append((i + skip, i))
            uniq = sorted(set(idx))
            if is_causal:
                uniq = [(r, c) for r, c in uniq if r >= c]
            uniq = uniq[:keep]
            rows = np.array([r for r, c in uniq], dtype=np.int32)
            cols = np.array([c for r, c in uniq], dtype=np.int32)
            return (rows, cols)
        ROWS, COLS = _block_pattern(SEQ, BLOCK, SPARSITY, is_causal=False)
        B, S, E = query.shape
        nb = S // BLOCK
        scale = HEAD_DIM ** (-0.5)

        def proj_blocks(x, W):
            h = (x @ W.T).reshape(B, S, NUM_HEADS, HEAD_DIM).transpose(0, 2, 1, 3)
            return h.reshape(B, NUM_HEADS, nb, BLOCK, HEAD_DIM)
        qb = proj_blocks(query, Wq)
        kb = proj_blocks(key, Wk)
        vb = proj_blocks(value, Wv)
        rows = jnp.asarray(ROWS)
        cols = jnp.asarray(COLS)
        qg = qb[:, :, rows]
        kg = kb[:, :, cols]
        vg = vb[:, :, cols]
        scores = jnp.einsum('bhpqd,bhpkd->bhpqk', qg, kg) * scale
        attn = jax.nn.softmax(scores, axis=-1)
        ob = jnp.einsum('bhpqk,bhpkd->bhpqd', attn, vg)
        acc = jax.ops.segment_sum(ob.transpose(2, 0, 1, 3, 4), rows, num_segments=nb)
        out = acc.transpose(1, 2, 0, 3, 4).reshape(B, NUM_HEADS, S, HEAD_DIM)
        out = out.transpose(0, 2, 1, 3).reshape(B, S, E)
        return out @ Wo.T

    def _L0_ffn_ref(x, gate_w, w1, b1, w2, b2, sw1, sb1, sw2, sb2):
        import jax, jax.numpy as jnp
        import numpy as np
        D_MODEL = 256
        HIDDEN = 1024
        N_ROUTING = 2
        B, S, D = x.shape
        xf = x.reshape(-1, D)
        gate_scores = xf @ gate_w.T
        gate_probs = jax.nn.softmax(gate_scores, axis=-1)
        top1 = jnp.argmax(gate_probs, axis=-1)
        one_hot = jax.nn.one_hot(top1, N_ROUTING, dtype=xf.dtype)
        masked = xf[None, :, :] * one_hot.T[:, :, None]
        h = jax.nn.relu(jnp.einsum('end,edh->enh', masked, w1) + b1[:, None, :])
        expert_out = jnp.einsum('enh,ehd->end', h, w2) + b2[:, None, :]
        routing_output = expert_out.sum(axis=0)
        shared = jax.nn.relu(xf @ sw1 + sb1) @ sw2 + sb2
        return (routing_output + shared).reshape(B, S, D)
    x = x + _L0_xattn_ref(_layernorm(x, axis=-1), ctx_1024, ctx_1024, L0_xattn_Wq, L0_xattn_Wk, L0_xattn_Wv, L0_xattn_Wo)
    x = x + _L0_ffn_ref(_layernorm(x, axis=-1), L0_ffn_gate_w, L0_ffn_w1, L0_ffn_b1, L0_ffn_w2, L0_ffn_b2, L0_ffn_sw1, L0_ffn_sb1, L0_ffn_sw2, L0_ffn_sb2)
    return x

_drawn_inputs = setup_inputs


def setup_inputs(seed=0):
    import zlib

    import numpy as np

    out = dict(_drawn_inputs(seed))
    spreads = {}
    factors = {'L0_ffn_b1': 8.0, 'L0_ffn_b2': 6.892, 'L0_ffn_sb1': 23.105, 'L0_ffn_sb2': 8.0}
    for name, (base, spread) in spreads.items():
        noise = np.random.default_rng([zlib.crc32(name.encode()), seed]).standard_normal(out[name].shape)
        drawn = base * np.exp(spread * noise) if base else spread * noise
        out[name] = jnp.asarray(drawn.astype(out[name].dtype))
    for name, factor in factors.items():
        out[name] = (out[name] * factor).astype(out[name].dtype)
    return out
```

```python
from contextlib import ExitStack

import concourse.bass as bass
from concourse import mybir

ALU = mybir.AluOpType
ACT = mybir.ActivationFunctionType
AX_X = mybir.AxisListType.X
F32 = mybir.dt.float32
F32R = mybir.dt.float32r
BF16 = mybir.dt.bfloat16

P = 128
BATCH, SEQ, D = 16, 256, 256
HEADS, HD = 16, 16
PAIRS = HEADS // 2
BLOCK = 64
NBLK = SEQ // BLOCK
HIDDEN = 1024
EXPERTS = 3
DC = D // P
TT = SEQ // P
HT = HIDDEN // P
UNITS = EXPERTS * HT // 2
EPS = 1e-5
QSCALE = HD ** -0.5
SHIFT_ROW = 96
SROWS = 16

S_JOBS = [("s", j) for j in range(PAIRS * TT)]
ST_JOBS = [("st", j) for j in range(HEADS)]
FRONT_JOBS = [("xT", 0), ("q", 0), ("k", 0), ("v", 0)]
PREP_JOBS = [("x2T", 0), ("mk", 0)]
CORE_JOBS = S_JOBS + [("mT", 0)] + ST_JOBS + [("at", 0), ("wo", 0)]
CYCLE = CORE_JOBS + FRONT_JOBS + PREP_JOBS
WORK_BANKS = 3
BANK = {job: n % WORK_BANKS for n, job in enumerate(CYCLE)}
EVACUATED = {"s": ("max_done", PAIRS * TT), "st": ("exp_done", HEADS), "mT": ("m_lo", 1), "at": ("at_lo", 1),
             "wo": ("x1_done", 1), "xT": ("xT_lo", 1), "q": ("q_lo", 1), "k": ("k_lo", 1), "v": ("v_copied", 1),
             "x2T": ("x2_lo", 1), "mk": ("mask_copied", 1)}

SEMS = (
    "consts_loaded stage_loaded0 stage_loaded1 x_loaded ctx_loaded q_bounced k_bounced q_spread k_spread "
    "m_bounced shift_spread out_done "
    "xT_full q_full k_full v_full s_full mT_full st_full pv_done o_full at_full wo_full x2T_full mk_full "
    "hid_full w2_done "
    "xT_hi q_hi k_hi c_hi v_copied mT_hi exp_done at_hi x2_hi mask_copied relu_done stage_hi "
    "bias_summed consts_made ln1_step ln2_step gate_step ln1_done xT_lo q_lo k_lo max_done m_lo inverted t_done at_lo x1_done ln2_done "
    "diag_done x2_lo x2_step x2_masked y_done stage_lo "
    "zeroed veps1_done veps2_done rstd1_done rstd2_done c_lo tm_done hl_done xres_done x1b_done"
).split()


def R(ap):
    return ap.bitcast(F32R)


def xattn_ffn(nc, x, ctxT, wT, w1, w2, b1, b2, gate_w, ident, indicator, blocksum, multiplicity, headsum, out):
    with ExitStack() as ctx:
        def sb(name, shape, dt=F32):
            return ctx.enter_context(nc.sbuf_tensor(name, shape, dt))

        def ps(name, shape):
            return ctx.enter_context(nc.psum_tensor(name, shape, F32))

        sem = {name: ctx.enter_context(nc.semaphore(name)) for name in SEMS}

        wp_hi, wp_lo = sb("wp_hi", [P, 4, DC, D]), sb("wp_lo", [P, 4, DC, D])
        w1_hi, w1_lo = sb("w1_hi", [P, EXPERTS, DC, HIDDEN]), sb("w1_lo", [P, EXPERTS, DC, HIDDEN])
        w2_hi, w2_lo = sb("w2_hi", [P, EXPERTS * HT, D]), sb("w2_lo", [P, EXPERTS * HT, D])
        id32, id16, ones16 = sb("id32", [P, P]), sb("id16", [P, P], BF16), sb("ones16", [P, P], BF16)
        bias1 = sb("bias1", [P, EXPERTS * HT])
        bias2 = sb("bias2", [P, D])
        gate = sb("gate", [P, 2, D])
        bsum, hsum, mult = sb("bsum", [P, 32]), sb("hsum", [P, 32]), sb("mult", [P, SEQ])
        xin, x1, x1b = (sb(n, [P, TT, D]) for n in ("xin", "x1", "x1b"))
        xhat = sb("xhat", [P, TT, D])
        ctx_in = sb("ctx_in", [P, DC, SEQ])
        c_hi, c_lo = sb("c_hi_t", [P, DC, SEQ]), sb("c_lo_t", [P, DC, SEQ])
        a_hi, a_lo = sb("a_hi_t", [P, DC, SEQ]), sb("a_lo_t", [P, DC, SEQ])
        T = sb("T", [P, PAIRS, SEQ])
        qn = T[:, 0:4, :].rearrange("p (part c) t -> p part c t", part=2)
        kn = T[:, 4:8, :].rearrange("p (part c) t -> p part c t", part=2)
        QP, KP = sb("QP", [P, PAIRS, SEQ]), sb("KP", [P, PAIRS, 2, SEQ])
        V = sb("V", [P, TT, HEADS, 32])
        PT = sb("PT", [P, 4, TT, SEQ])
        nmax = sb("nmax", [P, TT, HEADS * NBLK])
        mT = sb("mT", [P, 2, P])
        X2 = sb("X2", [P, EXPERTS, 2, DC, SEQ])
        maskT = sb("maskT", [P, SEQ])
        diag = sb("diag", [P, TT, P], BF16)
        h32, hh, hl = (sb(n, [P, 2, 2, SEQ]) for n in ("h32", "hh", "hl"))
        stats, mv, rstd = sb("stats", [P, 2, TT, 6]), sb("mv", [P, 2, TT, 2]), sb("rstd", [P, 2, TT])
        veps, eps, power = sb("veps", [P, 2, TT]), sb("eps", [P, TT]), sb("power", [P, TT])
        pause = sb("pause", [1, 1])
        gsc, mask = sb("gsc", [P, 2, TT]), sb("mask", [P, TT])

        work = ps("work", [P, WORK_BANKS, 512])
        num, den = ps("num", [P, 2, SEQ]), ps("den", [P, 2, SEQ])
        hid, acc = ps("hid", [P, 2, 2, SEQ]), ps("acc", [P, TT, D])

        scratch_q = nc.dram_tensor("scratch_q", [2, D, SEQ], F32, kind="Internal").ap()
        scratch_k = nc.dram_tensor("scratch_k", [2, D, SEQ], F32, kind="Internal").ap()
        scratch_m = nc.dram_tensor("scratch_m", [2, HEADS * NBLK, SEQ], F32, kind="Internal").ap()

        def w1_piece(w, n):
            e, c, half = n // 4, n // 2 % 2, n % 2
            return w[:, e, c, 512 * half:512 * half + 512]

        def w2_piece(w, n):
            return w[:, 2 * n:2 * n + 2, :]

        proj_pieces = [(wT[n], wp_hi[:, n], wp_lo[:, n]) for n in range(4)]
        ffn_pieces = [(w1_piece(w1, n), w1_piece(w1_hi, n), w1_piece(w1_lo, n)) for n in range(12)]
        ffn_pieces += [(w2_piece(w2, n), w2_piece(w2_hi, n), w2_piece(w2_lo, n)) for n in range(12)]
        pieces = proj_pieces + ffn_pieces

        def stage(n, like):
            s = h32[:, n % 2].rearrange("p a t -> p (a t)")
            return s.rearrange("p (a b) -> p a b", a=2) if len(like.shape) == 3 else s

        def unit_pieces(u):
            return range(len(proj_pieces) + 2 * u, len(proj_pieces) + 2 * u + 2)

        block = ctx.enter_context(nc.Block())

        @block.sync
        def _(sp):
            def load_piece(n):
                if n >= 2:
                    sp.wait_ge(sem["stage_lo"], n - 1)
                sp.dma_start(stage(n, pieces[n][0]), pieces[n][0]).then_inc(sem[f"stage_loaded{n % 2}"], 16)

            def load_x(n, first=False):
                if not first:
                    sp.wait_ge(sem["xres_done"], n)
                    sp.wait_ge(sem["ln1_done"], n)
                sp.dma_start(xin[:, :, :], x[n].rearrange("(t p) d -> p t d", p=P)).then_inc(sem["x_loaded"], 16)

            def load_ctx(n, first=False):
                if not first:
                    sp.wait_ge(sem["c_lo"], n)
                sp.dma_start(ctx_in[:, :, :], ctxT[n].rearrange("(c p) t -> p c t", p=P)) \
                    .then_inc(sem["ctx_loaded"], 16)

            def bounce(n, part_done, parts, scratch, done):
                sp.wait_ge(sem[part_done], n + 1)
                sp.dma_start(scratch.rearrange("h (c p) t -> p h c t", p=P), parts).then_inc(sem[done], 16)

            def spread(n):
                sp.wait_ge(sem["q_bounced"], 16 * n + 16)
                for slot, part in enumerate((0, 1, 0)):
                    src = scratch_q[part].rearrange("(p s d) t -> s d p t", s=2, d=HD)
                    for s in range(2):
                        r = 48 * s + 16 * slot
                        sp.dma_start(QP[r:r + HD, :, :], src[s]).then_inc(sem["q_spread"], 16)
                sp.wait_ge(sem["k_bounced"], 16 * n + 16)
                for slot, part in enumerate((0, 0, 1)):
                    src = scratch_k[part].rearrange("(p s d) t -> s d p t", s=2, d=HD)
                    for s in range(2):
                        r = 48 * s + 16 * slot
                        sp.dma_start(KP[r:r + HD, :, s, :], src[s]).then_inc(sem["k_spread"], 16)

            def front(n):
                bounce(n, "q_lo", qn, scratch_q, "q_bounced")
                bounce(n, "k_lo", kn, scratch_k, "k_bounced")
                spread(n)

            def shift(n):
                sp.wait_ge(sem["m_lo"], n + 1)
                rows = HEADS * NBLK
                for t in range(TT):
                    sp.dma_start(scratch_m[:, :, P * t:P * t + P].rearrange("h r q -> r h q"),
                                 mT[rows * t:rows * t + rows, :, :]).then_inc(sem["m_bounced"], 16)
                sp.wait_ge(sem["m_bounced"], 32 * n + 32)
                for part in range(2):
                    r = SHIFT_ROW + 8 * part
                    sp.dma_start(QP[r:r + 8, :, :], scratch_m[part].rearrange("(p r) t -> r p t", r=8)) \
                        .then_inc(sem["shift_spread"], 16)

            def store(n):
                sp.wait_ge(sem["y_done"], n + 1)
                sp.dma_start(out[n].rearrange("(t p) d -> p t d", p=P), x1b[:, :, :]).then_inc(sem["out_done"], 16)

            def iteration(i, ffn, more, last_load=False):
                if not ffn:
                    for n in (p for u in range(5) for p in unit_pieces(u)):
                        load_piece(n)
                shift(i)
                if not ffn:
                    for n in (p for u in range(5, UNITS) for p in unit_pieces(u)):
                        load_piece(n)
                if more:
                    front(i + 1)
                if ffn:
                    store(i - 1)
                if more and not last_load:
                    load_ctx(i + 2)
                    load_x(i + 2)

            load_x(0, first=True)
            load_piece(0)
            load_ctx(0, first=True)
            load_piece(1)
            for dst, src in ((id32[:, :], ident), (bias1[:, :], b1), (mult[:, :], multiplicity),
                             (bsum[:, :], blocksum), (hsum[:, :], headsum),
                             (T[SHIFT_ROW:SHIFT_ROW + SROWS, :, :], indicator[:, 0]),
                             (PT[SHIFT_ROW:SHIFT_ROW + SROWS, :, :, :].rearrange("r a b t -> r (a b) t"),
                              indicator[:, 1]),
                             (gate[:, :, :], bass.AP(tensor=gate_w.tensor, offset=0, ap=[[0, P], [D, 2], [1, D]])),
                             (x1b[:, 0, :], bass.AP(tensor=b2.tensor, offset=0, ap=[[0, P], [1, D]])),
                             (x1b[:, 1, :], bass.AP(tensor=b2.tensor, offset=D, ap=[[0, P], [1, D]])),
                             (bias2[:, :], bass.AP(tensor=b2.tensor, offset=2 * D, ap=[[0, P], [1, D]]))):
                sp.dma_start(dst, src).then_inc(sem["consts_loaded"], 16)
            load_piece(2)
            load_piece(3)
            front(0)
            load_ctx(1)
            load_x(1)
            iteration(0, False, True)
            with sp.Fori(1, BATCH - 2) as i:
                iteration(i, True, True)
            iteration(BATCH - 2, True, True, last_load=True)
            iteration(BATCH - 1, True, False)
            store(BATCH - 1)
            sp.wait_ge(sem["out_done"], 16 * BATCH)

        @block.tensor
        def _(pe):
            def claim(i, job, front=True):
                cycle = CYCLE if front else [j for j in CYCLE if j not in FRONT_JOBS]
                at = CYCLE.index(job)
                older = [j for j in CYCLE[:at] if BANK[j] == BANK[job] and j in cycle]
                if older:
                    name, count = EVACUATED[older[-1][0]]
                    k = i + 1 if older[-1] in FRONT_JOBS else i
                    pe.wait_ge(sem[name], k * count + older[-1][1] + 1)
                else:
                    last = [j for j in CYCLE if BANK[j] == BANK[job]][-1]
                    assert EVACUATED[last[0]][1] == 1
                    pe.wait_ge(sem[EVACUATED[last[0]][0]], i)
                return work[:, BANK[job], :]

            def split_product(dst, stat, mov, first=True, last=True):
                steps = [(s, m) for c in range(len(stat)) for s, m in
                         ((stat[c][0], mov[c][0]), (stat[c][0], mov[c][1]), (stat[c][1], mov[c][0]))]
                for n, (s, m) in enumerate(steps):
                    mm = nc.tensor.matmul(dst, R(s), R(m), start=first and n == 0, stop=last and n == len(steps) - 1)
                return mm

            def front_xT(n, bank=None):
                bank = claim(n - 1, ("xT", 0)) if bank is None else bank
                pe.wait_ge(sem["ln1_done"], n + 1)
                for c in range(DC):
                    for t in range(TT):
                        mm = nc.tensor.transpose(bank[:, SEQ * c + P * t:SEQ * c + P * t + P],
                                                 xhat[:, t, P * c:P * c + P], id32[:, :])
                mm.then_inc(sem["xT_full"], 1)

            def front_project(n, name, w, src_hi, src_lo, ready, bank=None):
                bank = claim(n - 1, (name, 0)) if bank is None else bank
                pe.wait_ge(sem[ready], n + 1)
                for o in range(DC):
                    cols = slice(P * o, P * o + P)
                    mm = split_product(bank[:, SEQ * o:SEQ * o + SEQ],
                                       [(wp_hi[:, w, c, cols], wp_lo[:, w, c, cols]) for c in range(DC)],
                                       [(src_hi[:, c, :], src_lo[:, c, :]) for c in range(DC)])
                mm.then_inc(sem[f"{name}_full"], 1)

            def front_v(n, bank=None):
                bank = claim(n - 1, ("v", 0)) if bank is None else bank
                for t in range(TT):
                    rows = slice(P * t, P * t + P)
                    mm = split_product(bank[:, D * t:D * t + D],
                                       [(c_hi[:, c, rows], c_lo[:, c, rows]) for c in range(DC)],
                                       [(wp_hi[:, 2, c, :], wp_lo[:, 2, c, :]) for c in range(DC)])
                mm.then_inc(sem["v_full"], 1)

            def scores(i, j):
                bank = claim(i, ("s", j))
                if j == 0:
                    pe.wait_ge(sem["q_spread"], 96 * i + 96)
                    pe.wait_ge(sem["k_spread"], 96 * i + 96)
                t, p = j // PAIRS, j % PAIRS
                nc.tensor.matmul(bank, R(QP[0:SHIFT_ROW, p, P * t:P * t + P]), R(KP[0:SHIFT_ROW, p, :, :]),
                                 start=True, stop=True).then_inc(sem["s_full"], 1)

            def maxima(i):
                bank = claim(i, ("mT", 0))
                pe.wait_ge(sem["max_done"], PAIRS * TT * (i + 1))
                nc.tensor.transpose(bank[:, 0:P], nmax[:, :, :].rearrange("q t r -> q (t r)"), id32[:, :]) \
                    .then_inc(sem["mT_full"], 1)

            def scores_t(i, j):
                bank = claim(i, ("st", j))
                if j == 0:
                    pe.wait_ge(sem["shift_spread"], 32 * i + 32)
                p, s = j // 2, j % 2
                for t in range(TT):
                    mm = nc.tensor.matmul(bank[:, SEQ * t:SEQ * t + SEQ], R(KP[:, p, s, P * t:P * t + P]),
                                          R(QP[:, p, :]), start=True, stop=True)
                mm.then_inc(sem["st_full"], 1)

            def values(i, p):
                if p == 0:
                    pe.wait_ge(sem["v_copied"], i + 1)
                if p % 2 == 0:
                    pe.wait_ge(sem["t_done"], 4 * i + p // 2)
                pe.wait_ge(sem["exp_done"], HEADS * i + 2 * p + 2)
                for dst, of_values in ((num, True), (den, False)):
                    for s in range(2):
                        for t in range(TT):
                            r = 32 * (2 * s + t)
                            mm = nc.tensor.matmul(dst[r:r + 32, p % 2, :],
                                                  V[:, t, 2 * p + s, :] if of_values else bsum[:, :],
                                                  PT[:, (2 * p + s) % 4, t, :], start=True, stop=True)
                            if of_values is False and r == 96:
                                mm.then_inc(sem["pv_done"], 1)

            def attention_out(i):
                bank = claim(i, ("at", 0))
                pe.wait_ge(sem["tm_done"], 4 * i + 4)
                for c in range(DC):
                    for q in range(4):
                        mm = nc.tensor.matmul(bank[32 * q:32 * q + 32, SEQ * c:SEQ * c + SEQ], hsum[:, :],
                                              T[:, 4 * c + q, :], start=True, stop=True)
                mm.then_inc(sem["at_full"], 1)

            def project_out(i):
                bank = claim(i, ("wo", 0))
                pe.wait_ge(sem["at_lo"], i + 1)
                for t in range(TT):
                    rows = slice(P * t, P * t + P)
                    mm = split_product(bank[:, D * t:D * t + D],
                                       [(a_hi[:, c, rows], a_lo[:, c, rows]) for c in range(DC)],
                                       [(wp_hi[:, 3, c, :], wp_lo[:, 3, c, :]) for c in range(DC)])
                mm.then_inc(sem["wo_full"], 1)

            def prep(i, front):
                bank = claim(i, ("x2T", 0), front)
                pe.wait_ge(sem["ln2_done"], i + 1)
                for c in range(DC):
                    for t in range(TT):
                        mm = nc.tensor.transpose(bank[:, SEQ * c + P * t:SEQ * c + P * t + P],
                                                 xhat[:, t, P * c:P * c + P], id32[:, :])
                mm.then_inc(sem["x2T_full"], 1)
                bank = claim(i, ("mk", 0), front)
                pe.wait_ge(sem["diag_done"], i + 1)
                nc.tensor.matmul(bank[:, 0:SEQ], ones16[:, :], diag[:, :, :], start=True, stop=True) \
                    .then_inc(sem["mk_full"], 1)

            def ffn_up(n, u):
                if u == 0:
                    pe.wait_ge(sem["x2_masked"], n + 1)
                if u >= 2:
                    pe.wait_ge(sem["relu_done"], UNITS * n + u - 1)
                for a in range(2):
                    e, t = (2 * u + a) // HT, (2 * u + a) % HT
                    cols = slice(P * t, P * t + P)
                    mm = split_product(hid[:, u % 2, a, :],
                                       [(w1_hi[:, e, c, cols], w1_lo[:, e, c, cols]) for c in range(DC)],
                                       [(X2[:, e, 0, c, :], X2[:, e, 1, c, :]) for c in range(DC)])
                mm.then_inc(sem["hid_full"], 1)

            def ffn_down(n, u):
                pe.wait_ge(sem["hl_done"], UNITS * n + u + 1)
                if u == 0 and type(n) is int and n > 0:
                    pe.wait_ge(sem["y_done"], n)
                for a in range(2):
                    for t in range(TT):
                        rows = slice(P * t, P * t + P)
                        for k, (h, w) in enumerate(((hh, w2_hi), (hh, w2_lo), (hl, w2_hi))):
                            mm = nc.tensor.matmul(acc[:, t, :], R(h[:, u % 2, a, rows]), R(w[:, 2 * u + a, :]),
                                                  start=(u == 0 and a == 0 and t == 0 and k == 0),
                                                  stop=(u == UNITS - 1 and a == 1 and k == 2),
                                                  skip_group_check=True)
                mm.then_inc(sem["w2_done"], 1)

            def unit(i, u, ffn):
                if ffn:
                    ffn_up(i - 1, u)
                    if u >= 1:
                        ffn_down(i - 1, u - 1)

            def iteration(i, ffn, more):
                for u in range(4):
                    for j in range(4 * u, 4 * u + 4):
                        scores(i, j)
                    unit(i, u, ffn)
                maxima(i)
                unit(i, 4, ffn)
                unit(i, 5, ffn)
                scores_t(i, 0)
                scores_t(i, 1)
                for p in range(PAIRS):
                    if p + 1 < PAIRS:
                        scores_t(i, 2 * p + 2)
                        scores_t(i, 2 * p + 3)
                    if p % 2 == 0:
                        unit(i, 6 + p // 2, ffn)
                    values(i, p)
                unit(i, 10, ffn)
                attention_out(i)
                unit(i, 11, ffn)
                project_out(i)
                if more:
                    front_xT(i + 1)
                    front_project(i + 1, "q", 0, a_hi, a_lo, "xT_lo")
                    front_project(i + 1, "k", 1, c_hi, c_lo, "c_lo")
                    front_v(i + 1)
                if ffn:
                    ffn_down(i - 1, UNITS - 1)
                prep(i, more)

            pe.wait_ge(sem["consts_made"], 1)
            pe.wait_ge(sem["zeroed"], 6)
            front_xT(0, work[:, 2, :])
            pe.wait_ge(sem["stage_lo"], len(proj_pieces))
            front_project(0, "q", 0, a_hi, a_lo, "xT_lo", num.rearrange("p a b -> p (a b)"))
            front_project(0, "k", 1, c_hi, c_lo, "c_lo", den.rearrange("p a b -> p (a b)"))
            front_v(0, acc.rearrange("p a b -> p (a b)"))
            for name in ("xT_lo", "q_lo", "k_lo", "v_copied"):
                pe.wait_ge(sem[name], 1)
            iteration(0, False, True)
            pe.wait_ge(sem["stage_lo"], len(pieces))
            with pe.Fori(1, BATCH - 1) as i:
                iteration(i, True, True)
            iteration(BATCH - 1, True, False)
            for u in range(UNITS):
                ffn_up(BATCH - 1, u)
                if u >= 1:
                    ffn_down(BATCH - 1, u - 1)
            ffn_down(BATCH - 1, UNITS - 1)

        @block.scalar
        def _(act):
            def high(i, full, src, dst, done, scale=1.0):
                act.wait_ge(sem[full], i + 1)
                nc.scalar.activation(R(dst), src, ACT.Copy, scale=scale).then_inc(sem[done], 1)

            def work_bank(name, shape="p (c t) -> p c t"):
                return work[:, BANK[(name, 0)], :].rearrange(shape, c=2)

            def two(tensor):
                return tensor[:, :, :]

            def front(n, src_x=None, src_q=None, src_k=None, src_v=None):
                high(n, "xT_full", work_bank("xT") if src_x is None else src_x, two(a_hi), "xT_hi")
                high(n, "q_full", work_bank("q") if src_q is None else src_q, qn[:, 0], "q_hi", QSCALE)
                high(n, "k_full", work_bank("k") if src_k is None else src_k, kn[:, 0], "k_hi")
                src_v = work_bank("v") if src_v is None else src_v
                act.wait_ge(sem["v_full"], n + 1)
                for b in range(2):
                    rows = slice(BLOCK * b, BLOCK * b + BLOCK)
                    last = nc.scalar.activation(V[rows, :, :, HD * b:HD * b + HD],
                                                src_v[rows].rearrange("p t (h d) -> p t h d", h=HEADS), ACT.Copy)
                last.then_inc(sem["v_copied"], 1)

            def context_high(n):
                act.wait_ge(sem["ctx_loaded"], 16 * n + 16)
                if type(n) is not int or n > 0:
                    act.wait_ge(sem["v_full"], n)
                nc.scalar.activation(R(c_hi[:, :, :]), ctx_in[:, :, :], ACT.Copy).then_inc(sem["c_hi"], 1)

            def keep_input(n, first=False):
                act.wait_ge(sem["x_loaded"], 16 * n + 16)
                if not first:
                    act.wait_ge(sem["x1b_done"], n)
                nc.scalar.activation(x1[:, :, :], xin[:, :, :], ACT.Copy).then_inc(sem["xres_done"], 1)

            def split_high(n):
                act.wait_ge(sem[f"stage_loaded{n % 2}"], 16 * (n // 2) + 16)
                nc.scalar.activation(R(pieces[n][1]), stage(n, pieces[n][1]), ACT.Copy).then_inc(sem["stage_hi"], 1)

            def exps(i, j):
                act.wait_ge(sem["st_full"], HEADS * i + j + 1)
                if j % 2 == 0:
                    act.wait_ge(sem["pv_done"], PAIRS * i + max(j // 2 - 1, 0))
                nc.scalar.activation(PT[:, j % 4].rearrange("p t q -> p (t q)"), work[:, BANK[("st", j)], :],
                                     ACT.Exp).then_inc(sem["exp_done"], 1)

            def relu(n, u):
                act.wait_ge(sem["hid_full"], UNITS * n + u + 1)
                if u >= 2:
                    act.wait_ge(sem["hl_done"], UNITS * n + u - 1)
                    act.wait_ge(sem["w2_done"], UNITS * n + u - 1)
                for a in range(2):
                    k = 2 * u + a
                    for dst in (h32[:, u % 2, a, :], R(hh[:, u % 2, a, :])):
                        last = nc.scalar.activation(dst, hid[:, u % 2, a, :], ACT.Relu, bias=bias1[:, k:k + 1])
                last.then_inc(sem["relu_done"], 1)

            def unit(i, u, ffn):
                if ffn:
                    relu(i - 1, u)
                else:
                    for n in unit_pieces(u):
                        split_high(n)

            def iteration(i, ffn, more):
                for u in range(5):
                    unit(i, u, ffn)
                high(i, "mT_full", work[:, BANK[("mT", 0)], 0:P], mT[:, 0, :], "mT_hi")
                unit(i, 5, ffn)
                exps(i, 0)
                exps(i, 1)
                for p in range(PAIRS):
                    if p + 1 < PAIRS:
                        exps(i, 2 * p + 2)
                        exps(i, 2 * p + 3)
                    if p % 2 == 0:
                        unit(i, 6 + p // 2, ffn)
                if more:
                    context_high(i + 1)
                unit(i, 10, ffn)
                high(i, "at_full", work_bank("at"), two(a_hi), "at_hi")
                unit(i, 11, ffn)
                if more:
                    front(i + 1)
                act.wait_ge(sem["x2T_full"], i + 1)
                nc.scalar.activation(R(X2[:, 2, 0]), work_bank("x2T"), ACT.Copy).then_inc(sem["x2_hi"], 1)
                act.wait_ge(sem["mk_full"], i + 1)
                nc.scalar.activation(maskT[:, :], work[:, BANK[("mk", 0)], 0:SEQ], ACT.Copy) \
                    .then_inc(sem["mask_copied"], 1)
                if more:
                    keep_input(i + 1)

            context_high(0)
            keep_input(0, first=True)
            for n in range(len(proj_pieces)):
                split_high(n)
            front(0, work[:, 2, :].rearrange("p (c t) -> p c t", c=2), num[:, :, :], den[:, :, :], acc[:, :, :])
            iteration(0, False, True)
            with act.Fori(1, BATCH - 1) as i:
                iteration(i, True, True)
            iteration(BATCH - 1, True, False)
            for u in range(UNITS):
                relu(BATCH - 1, u)

        @block.vector
        def _(dve):
            def low(i, hi_done, src, hi, dst, done, scale=1.0):
                dve.wait_ge(sem[hi_done], i + 1)
                nc.vector.scalar_tensor_tensor(out=R(dst), in0=src, scalar=scale, in1=hi, op0=ALU.mult,
                                               op1=ALU.subtract).then_inc(sem[done], 1)

            def work_bank(name):
                return work[:, BANK[(name, 0)], :].rearrange("p (c t) -> p c t", c=2)

            def layer_norm(i, src, which, step):
                for t in range(TT):
                    last = nc.vector.bn_stats(stats[:, which, t, :], src[:, t, :])
                last.then_inc(sem[step], 1)
                dve.wait_ge(sem[step], 2 * i + 1)
                nc.vector.memset(pause[0:1, :], 0.0)
                for t in range(TT):
                    last = nc.vector.bn_aggr(mv[:, which, t, :], stats[:, which, t, :])
                last.then_inc(sem[step], 1)
                dve.wait_ge(sem[f"rstd{which + 1}_done"], i + 1)
                for t in range(TT):
                    last = nc.vector.tensor_scalar(xhat[:, t, :], src[:, t, :], mv[:, which, t, 0:1],
                                                   rstd[:, which, t:t + 1], ALU.subtract, ALU.mult)
                return last

            def norm1(n, first=False):
                dve.wait_ge(sem["x_loaded"], 16 * n + 16)
                if not first:
                    dve.wait_ge(sem["x2T_full"], n - 1)
                layer_norm(n, xin, 0, "ln1_step").then_inc(sem["ln1_done"], 1)

            def front_xT(n, src=None):
                low(n, "xT_hi", work_bank("xT") if src is None else src, a_hi[:, :, :], a_lo[:, :, :], "xT_lo")

            def front_qk(n, src_q=None, src_k=None):
                low(n, "q_hi", work_bank("q") if src_q is None else src_q, qn[:, 0], qn[:, 1], "q_lo", QSCALE)
                low(n, "k_hi", work_bank("k") if src_k is None else src_k, kn[:, 0], kn[:, 1], "k_lo")

            def maximum(i, j):
                dve.wait_ge(sem["s_full"], PAIRS * TT * i + j + 1)
                t, p = j // PAIRS, j % PAIRS
                nc.vector.tensor_reduce(nmax[:, t, 8 * p:8 * p + 8],
                                        work[:, BANK[("s", j)], :].rearrange("q (b k) -> q b k", k=BLOCK),
                                        AX_X, ALU.max, negate=True).then_inc(sem["max_done"], 1)

            def divide(i, g):
                dve.wait_ge(sem["pv_done"], PAIRS * i + 2 * g + 2)
                if g == 0:
                    dve.wait_ge(sem["q_bounced"], 16 * i + 16)
                    dve.wait_ge(sem["k_bounced"], 16 * i + 16)
                pair = T[:, 2 * g:2 * g + 2, :]
                nc.vector.reciprocal(pair, den[:, :, :]).then_inc(sem["inverted"], 1)
                dve.wait_ge(sem["inverted"], 4 * i + g + 1)
                nc.vector.tensor_tensor(pair, num[:, :, :], pair, ALU.mult).then_inc(sem["t_done"], 1)

            def residual(i):
                dve.wait_ge(sem["wo_full"], i + 1)
                dve.wait_ge(sem["xres_done"], i + 1)
                nc.vector.tensor_tensor(x1[:, :, :], work_bank("wo"), x1[:, :, :], ALU.add) \
                    .then_inc(sem["x1_done"], 1)

            def norm2(i, more):
                if more:
                    dve.wait_ge(sem["xT_full"], i + 2)
                dve.wait_ge(sem["x1_done"], i + 1)
                layer_norm(i, x1, 1, "ln2_step").then_inc(sem["ln2_done"], 1)

            def route(i):
                dve.wait_ge(sem["ln2_done"], i + 1)
                for e in range(2):
                    for t in range(TT):
                        last = nc.vector.tensor_tensor_reduce(
                            out=PT[:, e, t, :], in0=xhat[:, t, :], in1=gate[:, e, :], scale=1.0, scalar=0.0,
                            op0=ALU.mult, op1=ALU.add, accum_out=gsc[:, e, t:t + 1])
                last.then_inc(sem["gate_step"], 1)
                dve.wait_ge(sem["gate_step"], 2 * i + 1)
                nc.vector.tensor_tensor(mask[:, :], gsc[:, 1, :], gsc[:, 0, :], ALU.is_gt) \
                    .then_inc(sem["gate_step"], 1)
                dve.wait_ge(sem["gate_step"], 2 * i + 2)
                for t in range(TT):
                    last = nc.vector.tensor_scalar(diag[:, t, :], id16[:, :], mask[:, t:t + 1], None, ALU.mult)
                last.then_inc(sem["diag_done"], 1)

            def masked(i):
                low(i, "x2_hi", work_bank("x2T"), X2[:, 2, 0], X2[:, 2, 1], "x2_lo")
                dve.wait_ge(sem["x2_lo"], i + 1)
                dve.wait_ge(sem["mask_copied"], i + 1)
                shared, first, second = (X2[:, e].rearrange("p h c t -> p (h c) t") for e in (2, 0, 1))
                nc.vector.tensor_tensor(R(second), shared, maskT[:, None, :].to_broadcast([P, 2 * DC, SEQ]),
                                        ALU.mult).then_inc(sem["x2_step"], 1)
                dve.wait_ge(sem["x2_step"], i + 1)
                nc.vector.tensor_tensor(R(first), shared, second, ALU.subtract).then_inc(sem["x2_masked"], 1)

            def finish(n):
                dve.wait_ge(sem["w2_done"], UNITS * n + UNITS)
                dve.wait_ge(sem["x1b_done"], n + 1)
                nc.vector.tensor_tensor(x1b[:, :, :], acc[:, :, :], x1b[:, :, :], ALU.add) \
                    .then_inc(sem["y_done"], 1)

            def split_low(n):
                dve.wait_ge(sem["stage_hi"], n + 1)
                _, hi, lo = pieces[n]
                nc.vector.tensor_tensor(R(lo), stage(n, lo), hi, ALU.subtract).then_inc(sem["stage_lo"], 1)

            def unit(i, u, ffn):
                if not ffn:
                    for n in unit_pieces(u):
                        split_low(n)

            def iteration(i, ffn, more):
                for u in range(4):
                    for j in range(4 * u, 4 * u + 4):
                        maximum(i, j)
                    unit(i, u, ffn)
                unit(i, 4, ffn)
                low(i, "mT_hi", work[:, BANK[("mT", 0)], 0:P], mT[:, 0, :], mT[:, 1, :], "m_lo")
                unit(i, 5, ffn)
                if more:
                    norm1(i + 1)
                for g in range(PAIRS // 2):
                    unit(i, 6 + g, ffn)
                    divide(i, g)
                unit(i, 10, ffn)
                low(i, "at_hi", work_bank("at"), a_hi[:, :, :], a_lo[:, :, :], "at_lo")
                unit(i, 11, ffn)
                residual(i)
                if more:
                    front_xT(i + 1)
                norm2(i, more)
                if more:
                    front_qk(i + 1)
                route(i)
                masked(i)
                if ffn:
                    finish(i - 1)

            norm1(0, first=True)
            dve.wait_ge(sem["consts_loaded"], 16 * 11)
            dve.wait_ge(sem["zeroed"], 6)
            rows = slice(SHIFT_ROW, SHIFT_ROW + SROWS)
            nc.vector.tensor_copy(R(KP[rows, :, 0, :]), T[rows, :, :])
            nc.vector.tensor_copy(R(KP[rows, :, 1, :]), PT[rows].rearrange("r a b t -> r (a b) t"))
            nc.vector.tensor_copy(id16[:, :], id32[:, :])
            nc.vector.tensor_tensor(bias2[:, :], bias2[:, :], x1b[:, 0, :], ALU.add) \
                .then_inc(sem["bias_summed"], 1)
            dve.wait_ge(sem["bias_summed"], 1)
            nc.vector.tensor_tensor(bias2[:, :], bias2[:, :], x1b[:, 1, :], ALU.add) \
                .then_inc(sem["consts_made"], 1)
            for n in range(len(proj_pieces)):
                split_low(n)
            front_xT(0, work[:, 2, :].rearrange("p (c t) -> p c t", c=2))
            front_qk(0, num[:, :, :], den[:, :, :])
            iteration(0, False, True)
            with dve.Fori(1, BATCH - 1) as i:
                iteration(i, True, True)
            iteration(BATCH - 1, True, False)
            finish(BATCH - 1)

        @block.gpsimd
        def _(pool):
            def context_low(n):
                pool.wait_ge(sem["c_hi"], n + 1)
                nc.gpsimd.tensor_tensor(R(c_lo[:, :, :]), ctx_in[:, :, :], c_hi[:, :, :], ALU.subtract) \
                    .then_inc(sem["c_lo"], 1)

            def reciprocal_deviation(i, which):
                pool.wait_ge(sem[f"ln{which + 1}_step"], 2 * i + 2)
                nc.gpsimd.tensor_tensor(veps[:, which, :], mv[:, which, :, 1], eps[:, :], ALU.add) \
                    .then_inc(sem[f"veps{which + 1}_done"], 1)
                pool.wait_ge(sem[f"veps{which + 1}_done"], i + 1)
                nc.gpsimd.tensor_tensor(rstd[:, which, :], veps[:, which, :], power[:, :], ALU.pow) \
                    .then_inc(sem[f"rstd{which + 1}_done"], 1)

            def weigh(i, g):
                pool.wait_ge(sem["t_done"], 4 * i + g + 1)
                pair = T[:, 2 * g:2 * g + 2, :]
                nc.gpsimd.tensor_tensor(pair, pair, mult[:, None, :].to_broadcast([P, 2, SEQ]), ALU.mult) \
                    .then_inc(sem["tm_done"], 1)

            def hidden_low(n, u):
                pool.wait_ge(sem["relu_done"], UNITS * n + u + 1)
                nc.gpsimd.tensor_tensor(R(hl[:, u % 2]), h32[:, u % 2], hh[:, u % 2], ALU.subtract) \
                    .then_inc(sem["hl_done"], 1)

            def add_bias(i):
                pool.wait_ge(sem["x1_done"], i + 1)
                pool.wait_ge(sem["ln2_done"], i + 1)
                pool.wait_ge(sem["out_done"], 16 * i)
                nc.gpsimd.tensor_tensor(x1b[:, :, :], x1[:, :, :], bias2[:, None, :].to_broadcast([P, TT, D]),
                                        ALU.add).then_inc(sem["x1b_done"], 1)

            def unit(i, u, ffn):
                if ffn:
                    hidden_low(i - 1, u)

            def iteration(i, ffn, more):
                for u in range(6):
                    unit(i, u, ffn)
                if more:
                    reciprocal_deviation(i + 1, 0)
                for g in range(PAIRS // 2):
                    unit(i, 6 + g, ffn)
                    weigh(i, g)
                if more:
                    context_low(i + 1)
                unit(i, 10, ffn)
                unit(i, 11, ffn)
                reciprocal_deviation(i, 1)
                add_bias(i)

            for t in (KP, QP, V, ones16):
                whole = t[:, :] if t is ones16 else t[:, :, :, :] if t is not QP else t[:, :, :]
                nc.gpsimd.memset(whole, 1.0 if t is ones16 else 0.0).then_inc(sem["zeroed"], 1)
            nc.gpsimd.memset(power[:, :], -0.5).then_inc(sem["zeroed"], 1)
            nc.gpsimd.memset(eps[:, :], EPS).then_inc(sem["zeroed"], 1)
            pool.wait_ge(sem["zeroed"], 6)
            reciprocal_deviation(0, 0)
            context_low(0)
            iteration(0, False, True)
            with pool.Fori(1, BATCH - 1) as i:
                iteration(i, True, True)
            iteration(BATCH - 1, True, False)
            for u in range(UNITS):
                hidden_low(BATCH - 1, u)


def kernel(**inputs):
    import numpy as np
    import concourse.bacc as bacc
    from concourse.bass_utils import run_bass_kernel_spmd

    def lay(a):
        return np.ascontiguousarray(a)

    def cols(w):
        w = np.asarray(w)
        return w.reshape(-1, P, w.shape[-1]).transpose(1, 0, 2)

    pattern_blocks, band = 8, 3
    seen = np.zeros((NBLK, NBLK), np.float32)
    for r in range(NBLK):
        for c in range(pattern_blocks):
            if abs(r - c) <= band:
                seen[r, min(c, NBLK - 1)] += 1
    part = np.arange(P)
    multiplicity = np.repeat(seen.T[part // 16 % NBLK], BLOCK, axis=1)
    blocksum = (part[:, None] // BLOCK == np.arange(32)[None] // HD).astype(np.float32)
    headsum = ((part[:, None] // 64 == np.arange(32)[None] // HD)
               & (part[:, None] % HD == np.arange(32)[None] % HD)).astype(np.float32)
    indicator = np.zeros((2, 2, NBLK, 2, PAIRS, SEQ), np.float32)
    for s in range(2):
        for b in range(NBLK):
            indicator[:, s, b, s, :, BLOCK * b:BLOCK * b + BLOCK] = 1.0
    w1 = [inputs["L0_ffn_w1"][0], inputs["L0_ffn_w1"][1], inputs["L0_ffn_sw1"]]
    w2 = [inputs["L0_ffn_w2"][0], inputs["L0_ffn_w2"][1], inputs["L0_ffn_sw2"]]
    b1 = [inputs["L0_ffn_b1"][0], inputs["L0_ffn_b1"][1], inputs["L0_ffn_sb1"]]
    b2 = [inputs["L0_ffn_b2"][0], inputs["L0_ffn_b2"][1], inputs["L0_ffn_sb2"]]
    arrays = {
        "x": lay(inputs["x"]),
        "ctxT": lay(np.asarray(inputs["ctx_1024"]).transpose(0, 2, 1)),
        "wT": lay(np.stack([cols(np.asarray(inputs[f"L0_xattn_W{n}"]).T) for n in "qkvo"])),
        "w1": lay(np.stack([cols(w) for w in w1], axis=1)),
        "w2": lay(np.concatenate([cols(w) for w in w2], axis=1)),
        "b1": lay(np.concatenate([np.asarray(b).reshape(-1, P).T for b in b1], axis=1)),
        "b2": lay(np.stack([np.asarray(b) for b in b2])),
        "gate_w": lay(inputs["L0_ffn_gate_w"]),
        "ident": np.eye(P, dtype=np.float32),
        "indicator": lay(indicator.reshape(SROWS, 2, PAIRS, SEQ)),
        "blocksum": lay(blocksum),
        "multiplicity": lay(multiplicity),
        "headsum": lay(headsum),
    }
    nc = bacc.Bacc("TRN2", target_bir_lowering=False, num_devices=1)
    args = [nc.dram_tensor(name, a.shape, F32, kind="ExternalInput").ap() for name, a in arrays.items()]
    out = nc.dram_tensor("out", (BATCH, SEQ, D), F32, kind="ExternalOutput").ap()
    xattn_ffn(nc, *args, out)
    r = run_bass_kernel_spmd(nc, [arrays], core_ids=[0])
    return r.results[0]["out"]
```

```python
from contextlib import ExitStack

import concourse.bass as bass
from concourse import mybir

ALU = mybir.AluOpType
ACT = mybir.ActivationFunctionType
AX_X = mybir.AxisListType.X
F32 = mybir.dt.float32
F32R = mybir.dt.float32r
BF16 = mybir.dt.bfloat16

P = 128
BATCH, SEQ, D = 16, 256, 256
HEADS, HD = 16, 16
PAIRS = HEADS // 2
BLOCK = 64
NBLK = SEQ // BLOCK
HIDDEN = 1024
EXPERTS = 3
DC = D // P
TT = SEQ // P
HT = HIDDEN // P
UNITS = EXPERTS * HT // 2
PAIR_UNIT = {0: 6, 3: 7, 5: 8}
EPS = 1e-5
QSCALE = HD ** -0.5
SHIFT_ROW = 96
SROWS = 16

S_JOBS = [("s", j) for j in range(PAIRS * TT)]
ST_JOBS = [("st", j) for j in range(HEADS)]
NEXT_JOBS = [("xT", 0), ("k", 0), ("q", 0), ("v", 0)]
CYCLE = (S_JOBS + [("mT", 0)] + NEXT_JOBS[:3] + ST_JOBS
         + [("at", 0), ("wo", 0), NEXT_JOBS[3], ("x2T", 0), ("mk", 0)])
WORK_BANKS = 3
STAGES = 3
BANK = {job: n % WORK_BANKS for n, job in enumerate(CYCLE)}
EVACUATED = {"s": ("max_done", PAIRS * TT), "st": ("exp_done", HEADS), "mT": ("m_lo", 1), "at": ("at_lo", 1),
             "wo": ("x1_done", 1), "xT": ("xT_lo", 1), "q": ("q_lo", 1), "k": ("k_lo", 1), "v": ("v_copied", 1),
             "x2T": ("x2_lo", 1), "mk": ("mask_copied", 1)}

SEMS = (
    "consts_loaded stage_loaded0 stage_loaded1 stage_loaded2 x_loaded res_loaded ctx_loaded first_q_bounced first_k_bounced q_bounced k_bounced q_spread k_spread "
    "m_bounced shift_spread out_done "
    "xT_full q_full k_full v_full s_full mT_full st_full pv_done o_full at_full wo_full x2T_full mk_full "
    "hid_full w2_done "
    "xT_hi q_hi k_hi c_hi v_copied mT_hi exp_done at_hi x2_hi mask_copied relu_done stage_hi "
    "bias_summed consts_made ln1_step ln2_step gate_step ln1_done xT_lo q_lo k_lo max_done m_lo inverted t_done at_lo x1_done ln2_done "
    "diag_done x2_lo y_done stage_lo "
    "zeroed x2_step x2_masked veps1_done veps2_done rstd1_done rstd2_done c_lo hl_done x1b_done"
).split()


def R(ap):
    return ap.bitcast(F32R)


def xattn_ffn(nc, x, ctxT, wT, w1, w2, b1, b2, gate_w, ident, indicator, blocksum, headsum, out):
    with ExitStack() as ctx:
        def sb(name, shape, dt=F32):
            return ctx.enter_context(nc.sbuf_tensor(name, shape, dt))

        def ps(name, shape):
            return ctx.enter_context(nc.psum_tensor(name, shape, F32))

        sem = {name: ctx.enter_context(nc.semaphore(name)) for name in SEMS}

        wp_hi, wp_lo = sb("wp_hi", [P, 4, DC, D]), sb("wp_lo", [P, 4, DC, D])
        w1_hi, w1_lo = sb("w1_hi", [P, EXPERTS, DC, HIDDEN]), sb("w1_lo", [P, EXPERTS, DC, HIDDEN])
        w2_hi, w2_lo = sb("w2_hi", [P, EXPERTS * HT, D]), sb("w2_lo", [P, EXPERTS * HT, D])
        id32, id16, ones16 = sb("id32", [P, P]), sb("id16", [P, P], BF16), sb("ones16", [P, P], BF16)
        bias1 = sb("bias1", [P, EXPERTS * HT])
        bias2 = sb("bias2", [P, D])
        gate = sb("gate", [P, 2, D])
        bsum, hsum = sb("bsum", [P, 32]), sb("hsum", [P, NBLK, 32])
        xin, x1, x1b = (sb(n, [P, TT, D]) for n in ("xin", "x1", "x1b"))
        xhat = sb("xhat", [P, TT, D])
        ctx_in = sb("ctx_in", [P, DC, SEQ])
        c_hi, c_lo = sb("c_hi_t", [P, DC, SEQ]), sb("c_lo_t", [P, DC, SEQ])
        a_hi, a_lo = sb("a_hi_t", [P, DC, SEQ]), sb("a_lo_t", [P, DC, SEQ])
        T = sb("T", [P, PAIRS, SEQ])
        qn = T[:, 0:4, :].rearrange("p (part c) t -> p part c t", part=2)
        kn = T[:, 4:8, :].rearrange("p (part c) t -> p part c t", part=2)
        QP, KP = sb("QP", [P, PAIRS, SEQ]), sb("KP", [P, PAIRS, 2, SEQ])
        V = sb("V", [P, TT, HEADS, 32])
        PT = sb("PT", [P, 4, TT, SEQ])
        nmax = sb("nmax", [P, TT, HEADS * NBLK])
        mT = sb("mT", [P, 2, P])
        X2 = sb("X2", [P, EXPERTS, 2, DC, SEQ])
        maskT = sb("maskT", [P, SEQ])
        diag = sb("diag", [P, TT, P], BF16)
        h32, hh, hl = (sb(n, [P, 2, 2, SEQ]) for n in ("h32", "hh", "hl"))
        stats, mv, rstd = sb("stats", [P, 2, TT, 6]), sb("mv", [P, 2, TT, 2]), sb("rstd", [P, 2, TT])
        veps, eps, power = sb("veps", [P, 2, TT]), sb("eps", [P, TT]), sb("power", [P, TT])
        pause = sb("pause", [1, 1])
        gsc, mask = sb("gsc", [P, 2, TT]), sb("mask", [P, TT])

        work = ps("work", [P, WORK_BANKS, 512])
        nd = ps("nd", [P, 2, 2, SEQ])
        hid, acc = ps("hid", [P, 2, 2, SEQ]), ps("acc", [P, TT, D])

        scratch_q = nc.dram_tensor("scratch_q", [2, D, SEQ], F32, kind="Internal").ap()
        scratch_k = nc.dram_tensor("scratch_k", [2, D, SEQ], F32, kind="Internal").ap()
        scratch_m = nc.dram_tensor("scratch_m", [2, HEADS * NBLK, SEQ], F32, kind="Internal").ap()

        def w1_piece(w, n):
            e, c, half = n // 4, n // 2 % 2, n % 2
            return w[:, e, c, 512 * half:512 * half + 512]

        def w2_piece(w, n):
            return w[:, 2 * n:2 * n + 2, :]

        proj_pieces = [(wT[n], wp_hi[:, n], wp_lo[:, n]) for n in range(4)]
        ffn_pieces = [(w1_piece(w1, n), w1_piece(w1_hi, n), w1_piece(w1_lo, n)) for n in range(12)]
        ffn_pieces += [(w2_piece(w2, n), w2_piece(w2_hi, n), w2_piece(w2_lo, n)) for n in range(12)]
        pieces = proj_pieces + ffn_pieces

        def stage(n, like):
            s = (h32[:, 0], h32[:, 1], x1b[:, :, :])[n % STAGES].rearrange("p a t -> p (a t)")
            return s.rearrange("p (a b) -> p a b", a=2) if len(like.shape) == 3 else s

        def load(queue, n):
            if n >= STAGES:
                queue.wait_ge(sem["stage_lo"], n - STAGES + 1)
            queue.dma_start(stage(n, pieces[n][0]), pieces[n][0]).then_inc(sem[f"stage_loaded{n % STAGES}"], 16)

        def unit_pieces(u):
            return range(len(proj_pieces) + 2 * u, len(proj_pieces) + 2 * u + 2)

        block = ctx.enter_context(nc.Block())

        @block.sync
        def _(sp):
            def load_x(n, first=False):
                if not first:
                    sp.wait_ge(sem["ln1_done"], n)
                sp.dma_start(xin[:, :, :], x[n].rearrange("(t p) d -> p t d", p=P)).then_inc(sem["x_loaded"], 16)

            def load_residual(n, first=False):
                if not first:
                    sp.wait_ge(sem["x1b_done"], n)
                sp.dma_start(x1[:, :, :], x[n].rearrange("(t p) d -> p t d", p=P)).then_inc(sem["res_loaded"], 16)

            def load_ctx(n, first=False):
                if not first:
                    sp.wait_ge(sem["c_lo"], n)
                sp.dma_start(ctx_in[:, :, :], ctxT[n].rearrange("(c p) t -> p c t", p=P)) \
                    .then_inc(sem["ctx_loaded"], 16)

            def bounce(n, part_done, parts, scratch, done):
                sp.wait_ge(sem[part_done], n + 1)
                sp.dma_start(scratch.rearrange("h (c p) t -> p h c t", p=P), parts).then_inc(sem[done], 16)

            def spread(bounced, q_bounced, k_bounced):
                sp.wait_ge(sem[k_bounced], bounced)
                for slot, part in enumerate((0, 0, 1)):
                    src = scratch_k[part].rearrange("(p s d) t -> s d p t", s=2, d=HD)
                    for s in range(2):
                        r = 48 * s + 16 * slot
                        sp.dma_start(KP[r:r + HD, :, s, :], src[s]).then_inc(sem["k_spread"], 16)
                sp.wait_ge(sem[q_bounced], bounced)
                for slot, part in enumerate((0, 1, 0)):
                    src = scratch_q[part].rearrange("(p s d) t -> s d p t", s=2, d=HD)
                    for s in range(2):
                        r = 48 * s + 16 * slot
                        sp.dma_start(QP[r:r + HD, :, :], src[s]).then_inc(sem["q_spread"], 16)

            def bounces(n):
                bounce(n, "k_lo", kn, scratch_k, "k_bounced")
                bounce(n, "q_lo", qn, scratch_q, "q_bounced")

            def shift(n):
                sp.wait_ge(sem["m_lo"], n + 1)
                rows = HEADS * NBLK
                for t in range(TT):
                    sp.dma_start(scratch_m[:, :, P * t:P * t + P].rearrange("h r q -> r h q"),
                                 mT[rows * t:rows * t + rows, :, :]).then_inc(sem["m_bounced"], 16)
                sp.wait_ge(sem["m_bounced"], 32 * n + 32)
                for part in range(2):
                    r = SHIFT_ROW + 8 * part
                    sp.dma_start(QP[r:r + 8, :, :], scratch_m[part].rearrange("(p r) t -> r p t", r=8)) \
                        .then_inc(sem["shift_spread"], 16)

            def store(n):
                sp.wait_ge(sem["y_done"], n + 1)
                sp.dma_start(out[n].rearrange("(t p) d -> p t d", p=P), x1b[:, :, :]).then_inc(sem["out_done"], 16)

            def iteration(i, ffn, more, last_load=False):
                shift(i)
                if more:
                    bounces(i + 1)
                if ffn:
                    load_residual(i)
                if more:
                    assert HEADS == 16
                    sp.wait_ge(sem["st_full"], 16 * (i + 1))
                    spread(16 * (i + 1), "q_bounced", "k_bounced")
                if more and not last_load:
                    load_ctx(i + 2)
                    load_x(i + 2)
                if ffn:
                    store(i - 1)

            load_x(0, first=True)
            load_residual(0, first=True)
            load_ctx(0, first=True)
            for dst, src in ((id32[:, :], ident), (bias1[:, :], b1), 
                             (bsum[:, :], blocksum), (hsum[:, :, :], headsum),
                             (T[SHIFT_ROW:SHIFT_ROW + SROWS, :, :], indicator[:, 0]),
                             (PT[SHIFT_ROW:SHIFT_ROW + SROWS, :, :, :].rearrange("r a b t -> r (a b) t"),
                              indicator[:, 1]),
                             (gate[:, :, :], bass.AP(tensor=gate_w.tensor, offset=0, ap=[[0, P], [D, 2], [1, D]])),
                             (maskT[:, :], bass.AP(tensor=b2.tensor, offset=0, ap=[[0, P], [1, D]])),
                             (mT[:, :, :].rearrange("p a b -> p (a b)"), bass.AP(tensor=b2.tensor, offset=D, ap=[[0, P], [1, D]])),
                             (bias2[:, :], bass.AP(tensor=b2.tensor, offset=2 * D, ap=[[0, P], [1, D]]))):
                sp.dma_start(dst, src).then_inc(sem["consts_loaded"], 16)
            bounce(0, "k_lo", kn, scratch_k, "first_k_bounced")
            bounce(0, "q_lo", qn, scratch_q, "first_q_bounced")
            spread(16, "first_q_bounced", "first_k_bounced")
            load_ctx(1)
            load_x(1)
            iteration(0, False, True)
            with sp.Fori(1, BATCH - 2) as i:
                iteration(i, True, True)
            iteration(BATCH - 2, True, True, last_load=True)
            iteration(BATCH - 1, True, False)
            store(BATCH - 1)
            sp.wait_ge(sem["out_done"], 16 * BATCH)

        @block.tensor
        def _(pe):
            def claim(i, job, more=True):
                same = [j for j in CYCLE if BANK[j] == BANK[job] and (more or j not in NEXT_JOBS)]
                at = same.index(job)
                before, iteration = (same[at - 1], i) if at else (same[-1], i - 1)
                name, count = EVACUATED[before[0]]
                n = iteration + 1 if before in NEXT_JOBS else iteration
                value = n * count + before[1] + 1
                if type(value) is not int or value > 0:
                    pe.wait_ge(sem[name], value)
                return work[:, BANK[job], :]

            def split_product(dst, stat, mov, first=True, last=True):
                steps = [(s, m) for c in range(len(stat)) for s, m in
                         ((stat[c][0], mov[c][0]), (stat[c][0], mov[c][1]), (stat[c][1], mov[c][0]))]
                for n, (s, m) in enumerate(steps):
                    mm = nc.tensor.matmul(dst, R(s), R(m), start=first and n == 0, stop=last and n == len(steps) - 1)
                return mm

            def front_xT(n, bank=None):
                bank = claim(n - 1, ("xT", 0)) if bank is None else bank
                pe.wait_ge(sem["ln1_done"], n + 1)
                for c in range(DC):
                    for t in range(TT):
                        mm = nc.tensor.transpose(bank[:, SEQ * c + P * t:SEQ * c + P * t + P],
                                                 xhat[:, t, P * c:P * c + P], id32[:, :])
                mm.then_inc(sem["xT_full"], 1)

            def front_project(n, name, w, src_hi, src_lo, ready, bank=None):
                bank = claim(n - 1, (name, 0)) if bank is None else bank
                pe.wait_ge(sem[ready], n + 1)
                for o in range(DC):
                    cols = slice(P * o, P * o + P)
                    mm = split_product(bank[:, SEQ * o:SEQ * o + SEQ],
                                       [(wp_hi[:, w, c, cols], wp_lo[:, w, c, cols]) for c in range(DC)],
                                       [(src_hi[:, c, :], src_lo[:, c, :]) for c in range(DC)])
                mm.then_inc(sem[f"{name}_full"], 1)

            def front_v(n, bank=None):
                bank = claim(n - 1, ("v", 0)) if bank is None else bank
                for t in range(TT):
                    rows = slice(P * t, P * t + P)
                    mm = split_product(bank[:, D * t:D * t + D],
                                       [(c_hi[:, c, rows], c_lo[:, c, rows]) for c in range(DC)],
                                       [(wp_hi[:, 2, c, :], wp_lo[:, 2, c, :]) for c in range(DC)])
                mm.then_inc(sem["v_full"], 1)

            def scores(i, j):
                bank = claim(i, ("s", j))
                if j == 0:
                    pe.wait_ge(sem["q_spread"], 96 * i + 96)
                    pe.wait_ge(sem["k_spread"], 96 * i + 96)
                t, p = j // PAIRS, j % PAIRS
                nc.tensor.matmul(bank, R(QP[0:SHIFT_ROW, p, P * t:P * t + P]), R(KP[0:SHIFT_ROW, p, :, :]),
                                 start=True, stop=True).then_inc(sem["s_full"], 1)

            def maxima(i):
                bank = claim(i, ("mT", 0))
                pe.wait_ge(sem["max_done"], PAIRS * TT * (i + 1))
                nc.tensor.transpose(bank[:, 0:P], nmax[:, :, :].rearrange("q t r -> q (t r)"), id32[:, :]) \
                    .then_inc(sem["mT_full"], 1)

            def scores_t(i, j, more):
                bank = claim(i, ("st", j), more)
                if j == 0:
                    pe.wait_ge(sem["shift_spread"], 32 * i + 32)
                p, s = j // 2, j % 2
                for t in range(TT):
                    mm = nc.tensor.matmul(bank[:, SEQ * t:SEQ * t + SEQ], R(KP[:, p, s, P * t:P * t + P]),
                                          R(QP[:, p, :]), start=True, stop=True)
                mm.then_inc(sem["st_full"], 1)

            def values(i, p):
                if p == 0:
                    pe.wait_ge(sem["v_copied"], i + 1)
                if p >= 2:
                    pe.wait_ge(sem["t_done"], PAIRS * i + p - 1)
                pe.wait_ge(sem["exp_done"], HEADS * i + 2 * p + 2)
                for kind in range(2):
                    for s in range(2):
                        for t in range(TT):
                            r = 32 * (2 * s + t)
                            mm = nc.tensor.matmul(nd[r:r + 32, p % 2, kind, :],
                                                  V[:, t, 2 * p + s, :] if kind == 0 else bsum[:, :],
                                                  PT[:, (2 * p + s) % 4, t, :], start=True, stop=True)
                mm.then_inc(sem["pv_done"], 1)

            def attention_out(i, more):
                bank = claim(i, ("at", 0), more).rearrange("p (c t) -> p c t", c=DC)
                pe.wait_ge(sem["t_done"], PAIRS * (i + 1))
                pairs = T[:, :, :].rearrange("p (c q) t -> p q c t", c=DC)
                for r in range(NBLK):
                    queries = slice(BLOCK * r, BLOCK * r + BLOCK)
                    for q in range(4):
                        mm = nc.tensor.matmul(bank[32 * q:32 * q + 32, :, queries], hsum[:, r, :],
                                              pairs[:, q, :, queries], start=True, stop=True)
                mm.then_inc(sem["at_full"], 1)

            def project_out(i, more):
                bank = claim(i, ("wo", 0), more)
                pe.wait_ge(sem["at_lo"], i + 1)
                for t in range(TT):
                    rows = slice(P * t, P * t + P)
                    mm = split_product(bank[:, D * t:D * t + D],
                                       [(a_hi[:, c, rows], a_lo[:, c, rows]) for c in range(DC)],
                                       [(wp_hi[:, 3, c, :], wp_lo[:, 3, c, :]) for c in range(DC)])
                mm.then_inc(sem["wo_full"], 1)

            def prep_tokens(i, more):
                bank = claim(i, ("x2T", 0), more)
                pe.wait_ge(sem["ln2_done"], i + 1)
                for c in range(DC):
                    for t in range(TT):
                        mm = nc.tensor.transpose(bank[:, SEQ * c + P * t:SEQ * c + P * t + P],
                                                 xhat[:, t, P * c:P * c + P], id32[:, :])
                mm.then_inc(sem["x2T_full"], 1)

            def prep_mask(i, more):
                bank = claim(i, ("mk", 0), more)
                pe.wait_ge(sem["diag_done"], i + 1)
                nc.tensor.matmul(bank[:, 0:SEQ], ones16[:, :], diag[:, :, :], start=True, stop=True) \
                    .then_inc(sem["mk_full"], 1)

            def ffn_up(n, u):
                if u == 0:
                    pe.wait_ge(sem["x2_lo"], n + 1)
                if u == HT // 2:
                    pe.wait_ge(sem["x2_masked"], n + 1)
                if u >= 2:
                    pe.wait_ge(sem["relu_done"], UNITS * n + u - 1)
                for a in range(2):
                    e, t = (2 * u + a) // HT, (2 * u + a) % HT
                    cols = slice(P * t, P * t + P)
                    mm = split_product(hid[:, u % 2, a, :],
                                       [(w1_hi[:, e, c, cols], w1_lo[:, e, c, cols]) for c in range(DC)],
                                       [(X2[:, e, 0, c, :], X2[:, e, 1, c, :]) for c in range(DC)])
                mm.then_inc(sem["hid_full"], 1)

            def ffn_down(n, u):
                pe.wait_ge(sem["hl_done"], UNITS * n + u + 1)
                if u == 0 and type(n) is int and n > 0:
                    pe.wait_ge(sem["y_done"], n)
                for a in range(2):
                    for t in range(TT):
                        rows = slice(P * t, P * t + P)
                        for k, (h, w) in enumerate(((hh, w2_hi), (hh, w2_lo), (hl, w2_hi))):
                            mm = nc.tensor.matmul(acc[:, t, :], R(h[:, u % 2, a, rows]), R(w[:, 2 * u + a, :]),
                                                  start=(u == 0 and a == 0 and t == 0 and k == 0),
                                                  stop=(u == UNITS - 1 and a == 1 and k == 2),
                                                  skip_group_check=True)
                mm.then_inc(sem["w2_done"], 1)

            def iteration(i, ffn, more):
                def up(u):
                    if ffn:
                        ffn_up(i - 1, u)

                def down(u):
                    if ffn and u >= 0:
                        ffn_down(i - 1, u)

                for u in range(4):
                    up(u)
                    scores(i, 4 * u)
                    scores(i, 4 * u + 1)
                    down(u - 1)
                    scores(i, 4 * u + 2)
                    scores(i, 4 * u + 3)
                up(4)
                maxima(i)
                down(3)
                if more:
                    front_xT(i + 1)
                up(5)
                if more:
                    front_project(i + 1, "k", 1, c_hi, c_lo, "c_lo")
                    front_project(i + 1, "q", 0, a_hi, a_lo, "xT_lo")
                down(4)
                scores_t(i, 0, more)
                scores_t(i, 1, more)
                for p in range(PAIRS):
                    if p in PAIR_UNIT:
                        up(PAIR_UNIT[p])
                    if p + 1 < PAIRS:
                        scores_t(i, 2 * p + 2, more)
                        scores_t(i, 2 * p + 3, more)
                    if p in PAIR_UNIT:
                        down(PAIR_UNIT[p] - 1)
                    values(i, p)
                up(9)
                down(8)
                attention_out(i, more)
                up(10)
                down(9)
                project_out(i, more)
                up(11)
                down(10)
                if more:
                    front_v(i + 1)
                prep_tokens(i, more)
                down(11)
                prep_mask(i, more)

            pe.wait_ge(sem["consts_made"], 1)
            pe.wait_ge(sem["zeroed"], 6)
            front_xT(0, work[:, 2, :])
            pe.wait_ge(sem["stage_lo"], len(proj_pieces))
            front_project(0, "k", 1, c_hi, c_lo, "c_lo", nd[:, 1].rearrange("p a b -> p (a b)"))
            front_project(0, "q", 0, a_hi, a_lo, "xT_lo", nd[:, 0].rearrange("p a b -> p (a b)"))
            front_v(0, acc.rearrange("p a b -> p (a b)"))
            for name in ("xT_lo", "q_lo", "k_lo", "v_copied"):
                pe.wait_ge(sem[name], 1)
            iteration(0, False, True)
            pe.wait_ge(sem["stage_lo"], len(pieces))
            with pe.Fori(1, BATCH - 1) as i:
                iteration(i, True, True)
            iteration(BATCH - 1, True, False)
            for u in range(UNITS):
                ffn_up(BATCH - 1, u)
                if u >= 1:
                    ffn_down(BATCH - 1, u - 1)
            ffn_down(BATCH - 1, UNITS - 1)

        @block.scalar
        def _(act):
            def high(i, full, src, dst, done, scale=1.0):
                act.wait_ge(sem[full], i + 1)
                nc.scalar.activation(R(dst), src, ACT.Copy, scale=scale).then_inc(sem[done], 1)

            def work_bank(name, shape="p (c t) -> p c t"):
                return work[:, BANK[(name, 0)], :].rearrange(shape, c=2)

            def two(tensor):
                return tensor[:, :, :]

            def front_x(n, src_x=None):
                high(n, "xT_full", work_bank("xT") if src_x is None else src_x, two(a_hi), "xT_hi")

            def front_qk(n, src_q=None, src_k=None):
                high(n, "k_full", work_bank("k") if src_k is None else src_k, kn[:, 0], "k_hi")
                high(n, "q_full", work_bank("q") if src_q is None else src_q, qn[:, 0], "q_hi", QSCALE)

            def front_v(n, src_v=None):
                src_v = work_bank("v") if src_v is None else src_v
                act.wait_ge(sem["v_full"], n + 1)
                for b in range(2):
                    rows = slice(BLOCK * b, BLOCK * b + BLOCK)
                    last = nc.scalar.activation(V[rows, :, :, HD * b:HD * b + HD],
                                                src_v[rows].rearrange("p t (h d) -> p t h d", h=HEADS), ACT.Copy)
                last.then_inc(sem["v_copied"], 1)

            def context_high(n):
                act.wait_ge(sem["ctx_loaded"], 16 * n + 16)
                if type(n) is not int or n > 0:
                    act.wait_ge(sem["v_full"], n)
                nc.scalar.activation(R(c_hi[:, :, :]), ctx_in[:, :, :], ACT.Copy).then_inc(sem["c_hi"], 1)

            def split_high(n):
                act.wait_ge(sem[f"stage_loaded{n % STAGES}"], 16 * (n // STAGES) + 16)
                nc.scalar.activation(R(pieces[n][1]), stage(n, pieces[n][1]), ACT.Copy).then_inc(sem["stage_hi"], 1)

            def exps(i, j):
                act.wait_ge(sem["st_full"], HEADS * i + j + 1)
                if j % 2 == 0:
                    act.wait_ge(sem["pv_done"], PAIRS * i + max(j // 2 - 1, 0))
                nc.scalar.activation(PT[:, j % 4].rearrange("p t q -> p (t q)"), work[:, BANK[("st", j)], :],
                                     ACT.Exp).then_inc(sem["exp_done"], 1)

            def relu(n, u):
                act.wait_ge(sem["hid_full"], UNITS * n + u + 1)
                if u >= 2:
                    act.wait_ge(sem["hl_done"], UNITS * n + u - 1)
                    act.wait_ge(sem["w2_done"], UNITS * n + u - 1)
                for a in range(2):
                    k = 2 * u + a
                    for dst in (h32[:, u % 2, a, :], R(hh[:, u % 2, a, :])):
                        last = nc.scalar.activation(dst, hid[:, u % 2, a, :], ACT.Relu, bias=bias1[:, k:k + 1])
                last.then_inc(sem["relu_done"], 1)

            def unit(i, u, ffn):
                if ffn:
                    relu(i - 1, u)
                else:
                    for n in unit_pieces(u):
                        split_high(n)

            def iteration(i, ffn, more):
                if more:
                    context_high(i + 1)
                for u in range(4):
                    unit(i, u, ffn)
                high(i, "mT_full", work[:, BANK[("mT", 0)], 0:P], mT[:, 0, :], "mT_hi")
                if more:
                    front_x(i + 1)
                unit(i, 4, ffn)
                if more:
                    front_qk(i + 1)
                unit(i, 5, ffn)
                exps(i, 0)
                exps(i, 1)
                for p in range(PAIRS):
                    if p in PAIR_UNIT:
                        unit(i, PAIR_UNIT[p], ffn)
                    if p + 1 < PAIRS:
                        exps(i, 2 * p + 2)
                        exps(i, 2 * p + 3)
                unit(i, 9, ffn)
                high(i, "at_full", work_bank("at"), two(a_hi), "at_hi")
                unit(i, 10, ffn)
                unit(i, 11, ffn)
                if more:
                    front_v(i + 1)
                act.wait_ge(sem["x2T_full"], i + 1)
                nc.scalar.activation(R(X2[:, 0, 0]), work_bank("x2T"), ACT.Copy).then_inc(sem["x2_hi"], 1)
                act.wait_ge(sem["mk_full"], i + 1)
                nc.scalar.activation(maskT[:, :], work[:, BANK[("mk", 0)], 0:SEQ], ACT.Copy) \
                    .then_inc(sem["mask_copied"], 1)

            context_high(0)
            for n in range(len(proj_pieces)):
                split_high(n)
            front_x(0, work[:, 2, :].rearrange("p (c t) -> p c t", c=2))
            front_qk(0, nd[:, 0], nd[:, 1])
            front_v(0, acc[:, :, :])
            iteration(0, False, True)
            with act.Fori(1, BATCH - 1) as i:
                iteration(i, True, True)
            iteration(BATCH - 1, True, False)
            for u in range(UNITS):
                relu(BATCH - 1, u)

        @block.vector
        def _(dve):
            def low(i, hi_done, src, hi, dst, done, scale=1.0):
                dve.wait_ge(sem[hi_done], i + 1)
                nc.vector.scalar_tensor_tensor(out=R(dst), in0=src, scalar=scale, in1=hi, op0=ALU.mult,
                                               op1=ALU.subtract).then_inc(sem[done], 1)

            def work_bank(name):
                return work[:, BANK[(name, 0)], :].rearrange("p (c t) -> p c t", c=2)

            def norm_stats(i, src, which):
                step = f"ln{which + 1}_step"
                for t in range(TT):
                    last = nc.vector.bn_stats(stats[:, which, t, :], src[:, t, :])
                last.then_inc(sem[step], 1)
                dve.wait_ge(sem[step], 2 * i + 1)
                nc.vector.memset(pause[0:1, :], 0.0)
                for t in range(TT):
                    last = nc.vector.bn_aggr(mv[:, which, t, :], stats[:, which, t, :])
                last.then_inc(sem[step], 1)

            def norm_apply(i, src, which):
                dve.wait_ge(sem[f"rstd{which + 1}_done"], i + 1)
                for t in range(TT):
                    last = nc.vector.tensor_scalar(xhat[:, t, :], src[:, t, :], mv[:, which, t, 0:1],
                                                   rstd[:, which, t:t + 1], ALU.subtract, ALU.mult)
                last.then_inc(sem[f"ln{which + 1}_done"], 1)

            def norm1_stats(n):
                dve.wait_ge(sem["x_loaded"], 16 * n + 16)
                norm_stats(n, xin, 0)

            def norm1_apply(n, first=False):
                if type(n) is not int or n > 1:
                    dve.wait_ge(sem["x2T_full"], n - 1)
                norm_apply(n, xin, 0)

            def front_xT(n, src=None):
                low(n, "xT_hi", work_bank("xT") if src is None else src, a_hi[:, :, :], a_lo[:, :, :], "xT_lo")

            def front_qk(n, src_q=None, src_k=None):
                low(n, "k_hi", work_bank("k") if src_k is None else src_k, kn[:, 0], kn[:, 1], "k_lo")
                low(n, "q_hi", work_bank("q") if src_q is None else src_q, qn[:, 0], qn[:, 1], "q_lo", QSCALE)

            def maximum(i, j):
                dve.wait_ge(sem["s_full"], PAIRS * TT * i + j + 1)
                t, p = j // PAIRS, j % PAIRS
                nc.vector.tensor_reduce(nmax[:, t, 8 * p:8 * p + 8],
                                        work[:, BANK[("s", j)], :].rearrange("q (b k) -> q b k", k=BLOCK),
                                        AX_X, ALU.max, negate=True).then_inc(sem["max_done"], 1)

            def divide(i, p):
                dve.wait_ge(sem["pv_done"], PAIRS * i + p + 1)
                nc.vector.reciprocal(T[:, p, :], nd[:, p % 2, 1, :]).then_inc(sem["inverted"], 1)
                dve.wait_ge(sem["inverted"], PAIRS * i + p + 1)
                nc.vector.tensor_tensor(T[:, p, :], nd[:, p % 2, 0, :], T[:, p, :], ALU.mult) \
                    .then_inc(sem["t_done"], 1)

            def residual(i):
                dve.wait_ge(sem["wo_full"], i + 1)
                dve.wait_ge(sem["res_loaded"], 16 * i + 16)
                nc.vector.tensor_tensor(x1[:, :, :], work_bank("wo"), x1[:, :, :], ALU.add) \
                    .then_inc(sem["x1_done"], 1)

            def norm2_stats(i):
                dve.wait_ge(sem["x1_done"], i + 1)
                norm_stats(i, x1, 1)

            def norm2_apply(i, more):
                if more:
                    dve.wait_ge(sem["xT_full"], i + 2)
                norm_apply(i, x1, 1)

            def route(i):
                dve.wait_ge(sem["ln2_done"], i + 1)
                for e in range(2):
                    for t in range(TT):
                        last = nc.vector.tensor_tensor_reduce(
                            out=PT[:, e, t, :], in0=xhat[:, t, :], in1=gate[:, e, :], scale=1.0, scalar=0.0,
                            op0=ALU.mult, op1=ALU.add, accum_out=gsc[:, e, t:t + 1])
                last.then_inc(sem["gate_step"], 1)
                dve.wait_ge(sem["gate_step"], 2 * i + 1)
                nc.vector.tensor_tensor(mask[:, :], gsc[:, 1, :], gsc[:, 0, :], ALU.is_gt) \
                    .then_inc(sem["gate_step"], 1)
                dve.wait_ge(sem["gate_step"], 2 * i + 2)
                for t in range(TT):
                    last = nc.vector.tensor_scalar(diag[:, t, :], id16[:, :], mask[:, t:t + 1], None, ALU.mult)
                last.then_inc(sem["diag_done"], 1)

            def shared_low(i):
                low(i, "x2_hi", work_bank("x2T"), X2[:, 0, 0], X2[:, 0, 1], "x2_lo")

            def finish(n):
                dve.wait_ge(sem["w2_done"], UNITS * n + UNITS)
                dve.wait_ge(sem["x1b_done"], n + 1)
                nc.vector.tensor_tensor(x1b[:, :, :], acc[:, :, :], x1b[:, :, :], ALU.add) \
                    .then_inc(sem["y_done"], 1)

            def split_low(n):
                dve.wait_ge(sem["stage_hi"], n + 1)
                _, hi, lo = pieces[n]
                nc.vector.tensor_tensor(R(lo), stage(n, lo), hi, ALU.subtract).then_inc(sem["stage_lo"], 1)

            def unit(i, u, ffn):
                if not ffn:
                    for n in unit_pieces(u):
                        split_low(n)

            def iteration(i, ffn, more):
                for u in range(4):
                    for j in range(4 * u, 4 * u + 4):
                        maximum(i, j)
                    unit(i, u, ffn)
                    if more and u == 1:
                        norm1_stats(i + 1)
                if more:
                    norm1_apply(i + 1)
                low(i, "mT_hi", work[:, BANK[("mT", 0)], 0:P], mT[:, 0, :], mT[:, 1, :], "m_lo")
                if more:
                    front_xT(i + 1)
                unit(i, 4, ffn)
                if more:
                    front_qk(i + 1)
                unit(i, 5, ffn)
                for p in range(PAIRS):
                    if p in PAIR_UNIT:
                        unit(i, PAIR_UNIT[p], ffn)
                    if p == 0:
                        dve.wait_ge(sem["q_bounced"], 16 * (i + more))
                        dve.wait_ge(sem["k_bounced"], 16 * (i + more))
                    divide(i, p)
                unit(i, 9, ffn)
                low(i, "at_hi", work_bank("at"), a_hi[:, :, :], a_lo[:, :, :], "at_lo")
                unit(i, 10, ffn)
                unit(i, 11, ffn)
                residual(i)
                norm2_stats(i)
                norm2_apply(i, more)
                route(i)
                shared_low(i)
                if ffn:
                    finish(i - 1)

            norm1_stats(0)
            norm1_apply(0)
            dve.wait_ge(sem["consts_loaded"], 16 * 10)
            dve.wait_ge(sem["zeroed"], 6)
            rows = slice(SHIFT_ROW, SHIFT_ROW + SROWS)
            nc.vector.tensor_copy(R(KP[rows, :, 0, :]), T[rows, :, :])
            nc.vector.tensor_copy(R(KP[rows, :, 1, :]), PT[rows].rearrange("r a b t -> r (a b) t"))
            nc.vector.tensor_copy(id16[:, :], id32[:, :])
            nc.vector.tensor_tensor(bias2[:, :], bias2[:, :], maskT[:, :], ALU.add) \
                .then_inc(sem["bias_summed"], 1)
            dve.wait_ge(sem["bias_summed"], 1)
            nc.vector.tensor_tensor(bias2[:, :], bias2[:, :], mT[:, :, :].rearrange("p a b -> p (a b)"), ALU.add) \
                .then_inc(sem["consts_made"], 1)
            for n in range(len(proj_pieces)):
                split_low(n)
            front_xT(0, work[:, 2, :].rearrange("p (c t) -> p c t", c=2))
            front_qk(0, nd[:, 0], nd[:, 1])
            iteration(0, False, True)
            with dve.Fori(1, BATCH - 1) as i:
                iteration(i, True, True)
            iteration(BATCH - 1, True, False)
            finish(BATCH - 1)

        @block.gpsimd
        def _(pool):
            def context_low(n):
                pool.wait_ge(sem["c_hi"], n + 1)
                nc.gpsimd.tensor_tensor(R(c_lo[:, :, :]), ctx_in[:, :, :], c_hi[:, :, :], ALU.subtract) \
                    .then_inc(sem["c_lo"], 1)

            def reciprocal_deviation(i, which):
                pool.wait_ge(sem[f"ln{which + 1}_step"], 2 * i + 2)
                nc.gpsimd.tensor_tensor(veps[:, which, :], mv[:, which, :, 1], eps[:, :], ALU.add) \
                    .then_inc(sem[f"veps{which + 1}_done"], 1)
                pool.wait_ge(sem[f"veps{which + 1}_done"], i + 1)
                nc.gpsimd.tensor_tensor(rstd[:, which, :], veps[:, which, :], power[:, :], ALU.pow) \
                    .then_inc(sem[f"rstd{which + 1}_done"], 1)

            def hidden_low(n, u):
                pool.wait_ge(sem["relu_done"], UNITS * n + u + 1)
                nc.gpsimd.tensor_tensor(R(hl[:, u % 2]), h32[:, u % 2], hh[:, u % 2], ALU.subtract) \
                    .then_inc(sem["hl_done"], 1)

            shared, first, second = (X2[:, e].rearrange("p h c t -> p (h c) t") for e in range(EXPERTS))

            def second_input(i):
                pool.wait_ge(sem["x2_lo"], i + 1)
                pool.wait_ge(sem["mask_copied"], i + 1)
                nc.gpsimd.tensor_tensor(R(second), shared, maskT[:, None, :].to_broadcast([P, 2 * DC, SEQ]),
                                        ALU.mult).then_inc(sem["x2_step"], 1)

            def first_input(i):
                pool.wait_ge(sem["x2_step"], i + 1)
                nc.gpsimd.tensor_tensor(R(first), shared, second, ALU.subtract).then_inc(sem["x2_masked"], 1)

            def add_bias(i):
                pool.wait_ge(sem["x1_done"], i + 1)
                pool.wait_ge(sem["ln2_done"], i + 1)
                pool.wait_ge(sem["out_done"], 16 * i)
                nc.gpsimd.tensor_tensor(x1b[:, :, :], x1[:, :, :], bias2[:, None, :].to_broadcast([P, TT, D]),
                                        ALU.add).then_inc(sem["x1b_done"], 1)

            def beside(n, u):
                if u == 0:
                    second_input(n)
                if u == 1:
                    first_input(n)
                if u == 3:
                    add_bias(n)

            def iteration(i, ffn, more):
                for u in range(UNITS):
                    if ffn and u == UNITS - 1:
                        reciprocal_deviation(i, 1)
                    if ffn:
                        hidden_low(i - 1, u)
                        beside(i - 1, u)
                    else:
                        for n in unit_pieces(u):
                            load(pool, n)
                    if more and u == 2:
                        reciprocal_deviation(i + 1, 0)
                        context_low(i + 1)
                if not ffn:
                    reciprocal_deviation(i, 1)

            for n in range(STAGES):
                load(pool, n)
            for t in (KP, QP, V, ones16):
                whole = t[:, :] if t is ones16 else t[:, :, :, :] if t is not QP else t[:, :, :]
                nc.gpsimd.memset(whole, 1.0 if t is ones16 else 0.0).then_inc(sem["zeroed"], 1)
            nc.gpsimd.memset(power[:, :], -0.5).then_inc(sem["zeroed"], 1)
            nc.gpsimd.memset(eps[:, :], EPS).then_inc(sem["zeroed"], 1)
            pool.wait_ge(sem["zeroed"], 6)
            reciprocal_deviation(0, 0)
            load(pool, STAGES)
            context_low(0)
            iteration(0, False, True)
            with pool.Fori(1, BATCH - 1) as i:
                iteration(i, True, True)
            iteration(BATCH - 1, True, False)
            for u in range(UNITS):
                hidden_low(BATCH - 1, u)
                beside(BATCH - 1, u)


def kernel(**inputs):
    import numpy as np
    import concourse.bacc as bacc
    from concourse.bass_utils import run_bass_kernel_spmd

    def lay(a):
        return np.ascontiguousarray(a)

    def cols(w):
        w = np.asarray(w)
        return w.reshape(-1, P, w.shape[-1]).transpose(1, 0, 2)

    pattern_blocks, band = 8, 3
    seen = np.zeros((NBLK, NBLK), np.float32)
    for r in range(NBLK):
        for c in range(pattern_blocks):
            if abs(r - c) <= band:
                seen[r, min(c, NBLK - 1)] += 1
    part = np.arange(P)
    blocksum = (part[:, None] // BLOCK == np.arange(32)[None] // HD).astype(np.float32)
    same = ((part[:, None] // 64 == np.arange(32)[None] // HD)
            & (part[:, None] % HD == np.arange(32)[None] % HD))
    headsum = seen.T[part // HD % NBLK][:, :, None] * same[:, None, :]
    indicator = np.zeros((2, 2, NBLK, 2, PAIRS, SEQ), np.float32)
    for s in range(2):
        for b in range(NBLK):
            indicator[:, s, b, s, :, BLOCK * b:BLOCK * b + BLOCK] = 1.0
    w1 = [inputs["L0_ffn_sw1"], inputs["L0_ffn_w1"][0], inputs["L0_ffn_w1"][1]]
    w2 = [inputs["L0_ffn_sw2"], inputs["L0_ffn_w2"][0], inputs["L0_ffn_w2"][1]]
    b1 = [inputs["L0_ffn_sb1"], inputs["L0_ffn_b1"][0], inputs["L0_ffn_b1"][1]]
    b2 = [inputs["L0_ffn_sb2"], inputs["L0_ffn_b2"][0], inputs["L0_ffn_b2"][1]]
    arrays = {
        "x": lay(inputs["x"]),
        "ctxT": lay(np.asarray(inputs["ctx_1024"]).transpose(0, 2, 1)),
        "wT": lay(np.stack([cols(np.asarray(inputs[f"L0_xattn_W{n}"]).T) for n in "qkvo"])),
        "w1": lay(np.stack([cols(w) for w in w1], axis=1)),
        "w2": lay(np.concatenate([cols(w) for w in w2], axis=1)),
        "b1": lay(np.concatenate([np.asarray(b).reshape(-1, P).T for b in b1], axis=1)),
        "b2": lay(np.stack([np.asarray(b) for b in b2])),
        "gate_w": lay(inputs["L0_ffn_gate_w"]),
        "ident": np.eye(P, dtype=np.float32),
        "indicator": lay(indicator.reshape(SROWS, 2, PAIRS, SEQ)),
        "blocksum": lay(blocksum),
        "headsum": lay(headsum),
    }
    nc = bacc.Bacc("TRN2", target_bir_lowering=False, num_devices=1)
    args = [nc.dram_tensor(name, a.shape, F32, kind="ExternalInput").ap() for name, a in arrays.items()]
    out = nc.dram_tensor("out", (BATCH, SEQ, D), F32, kind="ExternalOutput").ap()
    xattn_ffn(nc, *args, out)
    r = run_bass_kernel_spmd(nc, [arrays], core_ids=[0])
    return r.results[0]["out"]
```

```python
from contextlib import ExitStack

import concourse.bass as bass
from concourse import mybir

ALU = mybir.AluOpType
ACT = mybir.ActivationFunctionType
AX_X = mybir.AxisListType.X
F32 = mybir.dt.float32
F32R = mybir.dt.float32r
BF16 = mybir.dt.bfloat16

P = 128
BATCH, SEQ, D = 16, 256, 256
HEADS, HD = 16, 16
PAIRS = HEADS // 2
BLOCK = 64
NBLK = SEQ // BLOCK
HIDDEN = 1024
EXPERTS = 3
DC = D // P
TT = SEQ // P
HT = HIDDEN // P
UNITS = EXPERTS * HT // 2
EPS = 1e-5
QSCALE = HD ** -0.5
SHIFT_ROW = 96
SROWS = 16

SCORE_STEPS = ((0,), (1, 2, 3), (4, 5, 6), (7, 8), (9, 10), (11, 12, 13), (14, 15))
PAIR_UP = {0: 6, 3: 7, 6: 8}
PAIR_DOWN = {1: 5, 4: 6, 7: 7}
S_JOBS = [("s", j) for j in range(PAIRS * TT)]
ST_JOBS = [("st", j) for j in range(HEADS)]
NEXT_JOBS = [("xT", 0), ("k", 0), ("q", 0), ("v", 0)]
CYCLE = (S_JOBS + [("mT", 0)] + NEXT_JOBS[:3] + ST_JOBS
         + [("at", 0), ("wo", 0), ("x2T", 0), NEXT_JOBS[3], ("mk", 0)])
WORK_BANKS = 3
BANK = {job: n % WORK_BANKS for n, job in enumerate(CYCLE)}
BANK["mk", 0] = WORK_BANKS - 1
EVACUATED = {
    "s": ("max_done", PAIRS * TT), "mT": ("m_lo", 1),
    "xT": ("xT_lo", 1), "k": ("k_lo", 1), "q": ("q_lo", 1), "v": ("v_copied", 1),
    "st": ("exp_done", HEADS), "at": ("at_lo", 1), "wo": ("x1_done", 1),
    "x2T": ("x2_lo", 1), "mk": ("mask_copied", 1),
}

PROJ_ORDER = (1, 0, 2, 3)
W1_PIECES = EXPERTS * DC * HIDDEN // 512
W2_PIECES = EXPERTS * HT // 2
EARLY_PIECES = 4
STAGES, LATE_STAGES = 7, 3
SLOTS = [n % STAGES for n in range(2 * STAGES)]
SLOTS += [n % LATE_STAGES for n in range(W1_PIECES + W2_PIECES - len(SLOTS))]

SEMS = (
    "ident_loaded indicator_loaded consts_loaded proj_loaded0 proj_loaded1 proj_loaded2 proj_loaded3 "
    "stage_loaded0 stage_loaded1 stage_loaded2 stage_loaded3 stage_loaded4 stage_loaded5 stage_loaded6 "
    "x_loaded res_loaded ctx_loaded first_q_bounced first_k_bounced q_bounced k_bounced "
    "q_spread k_spread m_bounced shift_spread out_done "
    "xT_full q_full k_full v_full s_full mT_full st_full pv_done at_full wo_full x2T_full mk_full "
    "hid_full w2_done "
    "proj_hi xT_hi q_hi k_hi c_hi v_copied mT_hi exp_done at_hi x2_hi relu_done stage_hi "
    "bias_summed consts_made proj_lo stage_lo_dve ln1_step ln1_done ln2_step ln2_done xT_lo q_lo k_lo "
    "max_done m_lo inverted t_done at_lo x1_done gate_step diag_done mask_copied x2_lo y_done "
    "zeroed stage_lo_pool x2_step x2_masked veps1_done veps2_done rstd1_done rstd2_done c_lo hl_done x1b_done"
).split()


def R(ap):
    return ap.bitcast(F32R)


def flat(ap):
    return ap.rearrange("p a b -> p (a b)")


def xattn_ffn(nc, x, ctxT, wT, w1, w2, b1, b2, gate_w, ident, indicator, blocksum, headsum, out):
    with ExitStack() as ctx:
        def sb(name, shape, dt=F32):
            return ctx.enter_context(nc.sbuf_tensor(name, shape, dt))

        def ps(name, shape):
            return ctx.enter_context(nc.psum_tensor(name, shape, F32))

        sem = {name: ctx.enter_context(nc.semaphore(name)) for name in SEMS}

        wp_hi, wp_lo = sb("wp_hi", [P, 4, DC, D]), sb("wp_lo", [P, 4, DC, D])
        w1_hi, w1_lo = sb("w1_hi", [P, EXPERTS, DC, HIDDEN]), sb("w1_lo", [P, EXPERTS, DC, HIDDEN])
        w2_hi, w2_lo = sb("w2_hi", [P, EXPERTS * HT, D]), sb("w2_lo", [P, EXPERTS * HT, D])
        id32, id16, ones16 = sb("id32", [P, P]), sb("id16", [P, P], BF16), sb("ones16", [P, P], BF16)
        bias1 = sb("bias1", [P, EXPERTS * HT])
        bias2 = sb("bias2", [P, D])
        gate = sb("gate", [P, 2, D])
        bsum, hsum = sb("bsum", [P, 32]), sb("hsum", [P, NBLK, 32])
        xin, x1, x1b = (sb(n, [P, TT, D]) for n in ("xin", "x1", "x1b"))
        xhat = sb("xhat", [P, TT, D])
        ctx_in = sb("ctx_in", [P, DC, SEQ])
        c_hi, c_lo = sb("c_hi_t", [P, DC, SEQ]), sb("c_lo_t", [P, DC, SEQ])
        a_hi, a_lo = sb("a_hi_t", [P, DC, SEQ]), sb("a_lo_t", [P, DC, SEQ])
        T = sb("T", [P, PAIRS, SEQ])
        qn = T[:, 0:4, :].rearrange("p (part c) t -> p part c t", part=2)
        kn = T[:, 4:8, :].rearrange("p (part c) t -> p part c t", part=2)
        QP, KP = sb("QP", [P, PAIRS, SEQ]), sb("KP", [P, PAIRS, 2, SEQ])
        V = sb("V", [P, TT, HEADS, 32])
        PT = sb("PT", [P, 4, TT, SEQ])
        nmax = sb("nmax", [P, TT, HEADS * NBLK])
        mT = sb("mT", [P, 2, P])
        X2 = sb("X2", [P, EXPERTS, 2, DC, SEQ])
        maskT = sb("maskT", [P, SEQ])
        diag = sb("diag", [P, TT, P], BF16)
        h32, hh, hl = (sb(n, [P, 2, 2, SEQ]) for n in ("h32", "hh", "hl"))
        stats, mv, rstd = sb("stats", [P, 2, TT, 6]), sb("mv", [P, 2, TT, 2]), sb("rstd", [P, 2, TT])
        veps, eps, power = sb("veps", [P, 2, TT]), sb("eps", [P, TT]), sb("power", [P, TT])
        pause = sb("pause", [1, 1])
        gsc, mask = sb("gsc", [P, 2, TT]), sb("mask", [P, TT])

        work = ps("work", [P, WORK_BANKS, 512])
        nd = ps("nd", [P, 2, 2, SEQ])
        hid, acc = ps("hid", [P, 2, 2, SEQ]), ps("acc", [P, TT, D])

        scratch_q = nc.dram_tensor("scratch_q", [2, D, SEQ], F32, kind="Internal").ap()
        scratch_k = nc.dram_tensor("scratch_k", [2, D, SEQ], F32, kind="Internal").ap()
        scratch_m = nc.dram_tensor("scratch_m", [2, HEADS * NBLK, SEQ], F32, kind="Internal").ap()

        def w1_piece(w, n):
            e, c, half = n // 4, n // 2 % 2, n % 2
            return w[:, e, c, 512 * half:512 * half + 512]

        def w2_piece(w, n):
            return w[:, 2 * n:2 * n + 2, :]

        pieces = [(w1_piece(w1, n), w1_piece(w1_hi, n), w1_piece(w1_lo, n)) for n in range(W1_PIECES)]
        pieces += [(w2_piece(w2, n), w2_piece(w2_hi, n), w2_piece(w2_lo, n)) for n in range(W2_PIECES)]

        def stage(n, like):
            s = (h32[:, 0], h32[:, 1], x1b[:, :, :], *(PT[:, k] for k in range(4)))[SLOTS[n]]
            s = flat(s)
            return s.rearrange("p (a b) -> p a b", a=2) if len(like.shape) == 3 else s

        def loaded(n):
            return sem[f"stage_loaded{SLOTS[n]}"], 16 * SLOTS[:n + 1].count(SLOTS[n])

        def by_vector(n):
            return n % 2 == 1 and n < 2 * STAGES

        def low_done(n):
            return (sem["stage_lo_dve" if by_vector(n) else "stage_lo_pool"],
                    sum(by_vector(m) == by_vector(n) for m in range(n + 1)))

        def unit_pieces(u):
            n = EARLY_PIECES + 2 * (u - 1)
            return range(n, min(n + 2, len(pieces))) if u else ()

        shared, first, second = (X2[:, e].rearrange("p h c t -> p (h c) t") for e in range(EXPERTS))

        def second_input(engine, queue, i):
            queue.wait_ge(sem["x2_lo"], i + 1)
            queue.wait_ge(sem["mask_copied"], i + 1)
            engine.tensor_tensor(R(second), shared, maskT[:, None, :].to_broadcast([P, 2 * DC, SEQ]),
                                 ALU.mult).then_inc(sem["x2_step"], 1)

        def first_input(engine, queue, i):
            queue.wait_ge(sem["x2_step"], i + 1)
            engine.tensor_tensor(R(first), shared, second, ALU.subtract).then_inc(sem["x2_masked"], 1)

        block = ctx.enter_context(nc.Block())

        @block.sync
        def _(sp):
            def load_x(n, first=False):
                if not first:
                    sp.wait_ge(sem["ln1_done"], n)
                sp.dma_start(xin[:, :, :], x[n].rearrange("(t p) d -> p t d", p=P)).then_inc(sem["x_loaded"], 16)

            def load_residual(n, first=False):
                if not first:
                    sp.wait_ge(sem["x1b_done"], n)
                sp.dma_start(x1[:, :, :], x[n].rearrange("(t p) d -> p t d", p=P)).then_inc(sem["res_loaded"], 16)

            def load_ctx(n, first=False):
                if not first:
                    sp.wait_ge(sem["c_lo"], n)
                sp.dma_start(ctx_in[:, :, :], ctxT[n].rearrange("(c p) t -> p c t", p=P)) \
                    .then_inc(sem["ctx_loaded"], 16)

            def bounce(n, part_done, parts, scratch, done):
                sp.wait_ge(sem[part_done], n + 1)
                sp.dma_start(scratch.rearrange("h (c p) t -> p h c t", p=P), parts).then_inc(sem[done], 16)

            def spread(bounced, q_bounced, k_bounced):
                sp.wait_ge(sem[k_bounced], bounced)
                for slot, part in enumerate((0, 0, 1)):
                    src = scratch_k[part].rearrange("(p s d) t -> s d p t", s=2, d=HD)
                    for s in range(2):
                        r = 48 * s + 16 * slot
                        sp.dma_start(KP[r:r + HD, :, s, :], src[s]).then_inc(sem["k_spread"], 16)
                sp.wait_ge(sem[q_bounced], bounced)
                for slot, part in enumerate((0, 1, 0)):
                    src = scratch_q[part].rearrange("(p s d) t -> s d p t", s=2, d=HD)
                    for s in range(2):
                        r = 48 * s + 16 * slot
                        sp.dma_start(QP[r:r + HD, :, :], src[s]).then_inc(sem["q_spread"], 16)

            def bounces(n):
                bounce(n, "k_lo", kn, scratch_k, "k_bounced")
                bounce(n, "q_lo", qn, scratch_q, "q_bounced")

            def shift(n):
                sp.wait_ge(sem["m_lo"], n + 1)
                rows = HEADS * NBLK
                for t in range(TT):
                    sp.dma_start(scratch_m[:, :, P * t:P * t + P].rearrange("h r q -> r h q"),
                                 mT[rows * t:rows * t + rows, :, :]).then_inc(sem["m_bounced"], 16)
                sp.wait_ge(sem["m_bounced"], 32 * n + 32)
                for part in range(2):
                    r = SHIFT_ROW + 8 * part
                    sp.dma_start(QP[r:r + 8, :, :], scratch_m[part].rearrange("(p r) t -> r p t", r=8)) \
                        .then_inc(sem["shift_spread"], 16)

            def store(n):
                sp.wait_ge(sem["y_done"], n + 1)
                sp.dma_start(out[n].rearrange("(t p) d -> p t d", p=P), x1b[:, :, :]).then_inc(sem["out_done"], 16)

            def iteration(i, ffn, more, loads=True):
                shift(i)
                if more:
                    bounces(i + 1)
                if ffn:
                    load_residual(i)
                if more:
                    assert HEADS == 16
                    sp.wait_ge(sem["st_full"], 16 * (i + 1))
                    spread(16 * (i + 1), "q_bounced", "k_bounced")
                if more and loads:
                    load_ctx(i + 2)
                    load_x(i + 2)
                if ffn:
                    store(i - 1)

            def load_projection(n):
                w = PROJ_ORDER[n]
                sp.dma_start(PT[:, w], wT[w]).then_inc(sem[f"proj_loaded{n}"], 16)

            load_x(0, first=True)
            load_projection(0)
            load_ctx(0, first=True)
            sp.dma_start(id32[:, :], ident).then_inc(sem["ident_loaded"], 16)
            load_projection(1)
            load_projection(2)
            load_projection(3)
            sp.dma_start(x1[SHIFT_ROW:SHIFT_ROW + SROWS, :, :], indicator).then_inc(sem["indicator_loaded"], 16)
            for dst, src in ((bias1[:, :], b1), (bsum[:, :], blocksum), (hsum[:, :, :], headsum),
                             (gate[:, :, :], bass.AP(tensor=gate_w.tensor, offset=0, ap=[[0, P], [D, 2], [1, D]])),
                             (maskT[:, :], bass.AP(tensor=b2.tensor, offset=0, ap=[[0, P], [1, D]])),
                             (flat(mT), bass.AP(tensor=b2.tensor, offset=D, ap=[[0, P], [1, D]])),
                             (bias2[:, :], bass.AP(tensor=b2.tensor, offset=2 * D, ap=[[0, P], [1, D]]))):
                sp.dma_start(dst, src).then_inc(sem["consts_loaded"], 16)
            bounce(0, "k_lo", kn, scratch_k, "first_k_bounced")
            bounce(0, "q_lo", qn, scratch_q, "first_q_bounced")
            sp.wait_ge(sem["zeroed"], 6)
            spread(16, "first_q_bounced", "first_k_bounced")
            sp.wait_ge(sem["consts_made"], 1)
            load_residual(0, first=True)
            load_ctx(1)
            load_x(1)
            iteration(0, False, True)
            with sp.Fori(1, BATCH - 2) as i:
                iteration(i, True, True)
            iteration(BATCH - 2, True, True, loads=False)
            iteration(BATCH - 1, True, False)
            store(BATCH - 1)
            sp.wait_ge(sem["out_done"], 16 * BATCH)

        @block.tensor
        def _(pe):
            def claim(i, job, more=True):
                same = [j for j in CYCLE if BANK[j] == BANK[job] and (more or j not in NEXT_JOBS)]
                at = same.index(job)
                before, iteration = (same[at - 1], i) if at else (same[-1], i - 1)
                name, count = EVACUATED[before[0]]
                n = iteration + 1 if before in NEXT_JOBS else iteration
                value = n * count + before[1] + 1
                if type(value) is not int or value > 0:
                    pe.wait_ge(sem[name], value)
                return work[:, BANK[job], :]

            def split_product(dst, stat, mov):
                steps = [(s, m) for c in range(len(stat)) for s, m in
                         ((stat[c][0], mov[c][0]), (stat[c][0], mov[c][1]), (stat[c][1], mov[c][0]))]
                for n, (s, m) in enumerate(steps):
                    mm = nc.tensor.matmul(dst, R(s), R(m), start=n == 0, stop=n == len(steps) - 1)
                return mm

            def front_xT(n, bank=None):
                bank = claim(n - 1, ("xT", 0)) if bank is None else bank
                pe.wait_ge(sem["ln1_done"], n + 1)
                for c in range(DC):
                    for t in range(TT):
                        mm = nc.tensor.transpose(bank[:, SEQ * c + P * t:SEQ * c + P * t + P],
                                                 xhat[:, t, P * c:P * c + P], id32[:, :])
                mm.then_inc(sem["xT_full"], 1)

            def front_project(n, name, w, src_hi, src_lo, ready, bank=None):
                bank = claim(n - 1, (name, 0)) if bank is None else bank
                pe.wait_ge(sem[ready], n + 1)
                for o in range(DC):
                    cols = slice(P * o, P * o + P)
                    mm = split_product(bank[:, SEQ * o:SEQ * o + SEQ],
                                       [(wp_hi[:, w, c, cols], wp_lo[:, w, c, cols]) for c in range(DC)],
                                       [(src_hi[:, c, :], src_lo[:, c, :]) for c in range(DC)])
                mm.then_inc(sem[f"{name}_full"], 1)

            def front_v(n, bank=None):
                bank = claim(n - 1, ("v", 0)) if bank is None else bank
                for t in range(TT):
                    rows = slice(P * t, P * t + P)
                    mm = split_product(bank[:, D * t:D * t + D],
                                       [(c_hi[:, c, rows], c_lo[:, c, rows]) for c in range(DC)],
                                       [(wp_hi[:, 2, c, :], wp_lo[:, 2, c, :]) for c in range(DC)])
                mm.then_inc(sem["v_full"], 1)

            def scores(i, j):
                bank = claim(i, ("s", j))
                if j == 0:
                    pe.wait_ge(sem["q_spread"], 96 * i + 96)
                    pe.wait_ge(sem["k_spread"], 96 * i + 96)
                t, p = j // PAIRS, j % PAIRS
                nc.tensor.matmul(bank, R(QP[0:SHIFT_ROW, p, P * t:P * t + P]), R(KP[0:SHIFT_ROW, p, :, :]),
                                 start=True, stop=True).then_inc(sem["s_full"], 1)

            def maxima(i):
                bank = claim(i, ("mT", 0))
                pe.wait_ge(sem["max_done"], PAIRS * TT * (i + 1))
                nc.tensor.transpose(bank[:, 0:P], nmax[:, :, :].rearrange("q t r -> q (t r)"), id32[:, :]) \
                    .then_inc(sem["mT_full"], 1)

            def scores_t(i, j, more):
                bank = claim(i, ("st", j), more)
                if j == 0:
                    pe.wait_ge(sem["shift_spread"], 32 * i + 32)
                p, s = j // 2, j % 2
                for t in range(TT):
                    mm = nc.tensor.matmul(bank[:, SEQ * t:SEQ * t + SEQ], R(KP[:, p, s, P * t:P * t + P]),
                                          R(QP[:, p, :]), start=True, stop=True)
                mm.then_inc(sem["st_full"], 1)

            def values(i, p):
                if p == 0:
                    pe.wait_ge(sem["v_copied"], i + 1)
                if p >= 2:
                    pe.wait_ge(sem["t_done"], PAIRS * i + p - 1)
                pe.wait_ge(sem["exp_done"], HEADS * i + 2 * p + 2)
                for kind in range(2):
                    for s in range(2):
                        for t in range(TT):
                            r = 32 * (2 * s + t)
                            mm = nc.tensor.matmul(nd[r:r + 32, p % 2, kind, :],
                                                  V[:, t, 2 * p + s, :] if kind == 0 else bsum[:, :],
                                                  PT[:, (2 * p + s) % 4, t, :], start=True, stop=True)
                mm.then_inc(sem["pv_done"], 1)

            def attention_out(i, more):
                bank = claim(i, ("at", 0), more).rearrange("p (c t) -> p c t", c=DC)
                pe.wait_ge(sem["t_done"], PAIRS * (i + 1))
                pairs = T[:, :, :].rearrange("p (c q) t -> p q c t", c=DC)
                for r in range(NBLK):
                    queries = slice(BLOCK * r, BLOCK * r + BLOCK)
                    for q in range(4):
                        mm = nc.tensor.matmul(bank[32 * q:32 * q + 32, :, queries], hsum[:, r, :],
                                              pairs[:, q, :, queries], start=True, stop=True)
                mm.then_inc(sem["at_full"], 1)

            def project_out(i, more):
                bank = claim(i, ("wo", 0), more)
                wo_hi, wo_lo = wp_hi[:, 3], wp_lo[:, 3]
                for part, weights, ready in ((a_hi, (wo_hi, wo_lo), "at_hi"), (a_lo, (wo_hi,), "at_lo")):
                    pe.wait_ge(sem[ready], i + 1)
                    for t in range(TT):
                        for c in range(DC):
                            for w in weights:
                                first = part is a_hi and t == 0 and c == 0 and w is wo_hi
                                mm = nc.tensor.matmul(bank[:, D * t:D * t + D], R(part[:, c, P * t:P * t + P]),
                                                      R(w[:, c, :]), start=first,
                                                      stop=part is a_lo and c == DC - 1, skip_group_check=True)
                mm.then_inc(sem["wo_full"], 1)

            def prep_tokens(i, more):
                bank = claim(i, ("x2T", 0), more)
                pe.wait_ge(sem["ln2_done"], i + 1)
                for c in range(DC):
                    for t in range(TT):
                        mm = nc.tensor.transpose(bank[:, SEQ * c + P * t:SEQ * c + P * t + P],
                                                 xhat[:, t, P * c:P * c + P], id32[:, :])
                mm.then_inc(sem["x2T_full"], 1)

            def prep_mask(i, more):
                bank = claim(i, ("mk", 0), more)
                pe.wait_ge(sem["diag_done"], i + 1)
                nc.tensor.matmul(bank[:, 0:SEQ], ones16[:, :], diag[:, :, :], start=True, stop=True) \
                    .then_inc(sem["mk_full"], 1)

            def ffn_up(n, u):
                if u == 0:
                    pe.wait_ge(sem["x2_lo"], n + 1)
                if u == HT // 2:
                    pe.wait_ge(sem["x2_masked"], n + 1)
                if u >= 2:
                    pe.wait_ge(sem["relu_done"], 2 * (UNITS * n + u - 1))
                for a in range(2):
                    e, t = (2 * u + a) // HT, (2 * u + a) % HT
                    cols = slice(P * t, P * t + P)
                    mm = split_product(hid[:, u % 2, a, :],
                                       [(w1_hi[:, e, c, cols], w1_lo[:, e, c, cols]) for c in range(DC)],
                                       [(X2[:, e, 0, c, :], X2[:, e, 1, c, :]) for c in range(DC)])
                mm.then_inc(sem["hid_full"], 1)

            def ffn_down(n, u):
                if u == 0 and type(n) is int and n > 0:
                    pe.wait_ge(sem["y_done"], n)
                for h, parts, ready in ((hh, (w2_hi, w2_lo), "relu_done"), (hl, (w2_hi,), "hl_done")):
                    for a in range(2):
                        pe.wait_ge(sem[ready], 2 * (UNITS * n + u) + a + 1)
                        for t in range(TT):
                            for w in parts:
                                first = u == 0 and h is hh and a == 0 and t == 0 and w is w2_hi
                                mm = nc.tensor.matmul(acc[:, t, :], R(h[:, u % 2, a, P * t:P * t + P]),
                                                      R(w[:, 2 * u + a, :]), start=first,
                                                      stop=u == UNITS - 1 and h is hl and a == 1,
                                                      skip_group_check=True)
                mm.then_inc(sem["w2_done"], 1)

            def iteration(i, ffn, more):
                def up(u):
                    if ffn:
                        ffn_up(i - 1, u)

                def down(u):
                    if ffn:
                        ffn_down(i - 1, u)

                for step, jobs in enumerate(SCORE_STEPS):
                    for j in jobs:
                        scores(i, j)
                    if step % 2 == 0:
                        up(step // 2 + 1)
                    else:
                        down(step // 2)
                maxima(i)
                down(3)
                if more:
                    front_xT(i + 1)
                up(5)
                if more:
                    front_project(i + 1, "k", 1, c_hi, c_lo, "c_lo")
                    front_project(i + 1, "q", 0, a_hi, a_lo, "xT_lo")
                down(4)
                if not more:
                    up(6)
                    down(5)
                scores_t(i, 0, more)
                scores_t(i, 1, more)
                for p in range(PAIRS):
                    if p in PAIR_UP and (more or p > 0):
                        up(PAIR_UP[p])
                    if p in PAIR_DOWN and (more or p > 1):
                        down(PAIR_DOWN[p])
                    if p + 1 < PAIRS:
                        scores_t(i, 2 * p + 2, more)
                        scores_t(i, 2 * p + 3, more)
                    values(i, p)
                up(9)
                down(8)
                attention_out(i, more)
                up(10)
                project_out(i, more)
                down(9)
                up(11)
                down(10)
                prep_tokens(i, more)
                if more:
                    front_v(i + 1)
                down(11)
                if not ffn:
                    pe.wait_ge(*low_done(2 * STAGES - 1))
                    pe.wait_ge(*low_done(len(pieces) - 1))
                ffn_up(i, 0)
                prep_mask(i, more)

            pe.wait_ge(sem["ident_loaded"], 16)
            front_xT(0, work[:, 2, :])
            pe.wait_ge(sem["proj_lo"], 1)
            front_project(0, "k", 1, c_hi, c_lo, "c_lo", flat(nd[:, 1]))
            pe.wait_ge(sem["proj_lo"], 2)
            front_project(0, "q", 0, a_hi, a_lo, "xT_lo", flat(nd[:, 0]))
            pe.wait_ge(sem["proj_lo"], 3)
            front_v(0, flat(acc))
            pe.wait_ge(sem["consts_made"], 1)
            for name in ("xT_lo", "q_lo", "k_lo", "v_copied"):
                pe.wait_ge(sem[name], 1)
            iteration(0, False, True)
            with pe.Fori(1, BATCH - 1) as i:
                iteration(i, True, True)
            iteration(BATCH - 1, True, False)
            for u in range(1, UNITS):
                ffn_up(BATCH - 1, u)
                ffn_down(BATCH - 1, u - 1)
            ffn_down(BATCH - 1, UNITS - 1)

        @block.scalar
        def _(act):
            def high(i, full, src, dst, done, scale=1.0):
                act.wait_ge(sem[full], i + 1)
                nc.scalar.activation(R(dst), src, ACT.Copy, scale=scale).then_inc(sem[done], 1)

            def work_bank(name, shape="p (c t) -> p c t"):
                return work[:, BANK[(name, 0)], :].rearrange(shape, c=2)

            def front_x(n, src_x=None):
                high(n, "xT_full", work_bank("xT") if src_x is None else src_x, a_hi[:, :, :], "xT_hi")

            def front_qk(n, src_q=None, src_k=None):
                high(n, "k_full", work_bank("k") if src_k is None else src_k, kn[:, 0], "k_hi")
                high(n, "q_full", work_bank("q") if src_q is None else src_q, qn[:, 0], "q_hi", QSCALE)

            def front_v(n, src_v=None):
                src_v = work_bank("v") if src_v is None else src_v
                act.wait_ge(sem["v_full"], n + 1)
                for b in range(2):
                    rows = slice(BLOCK * b, BLOCK * b + BLOCK)
                    last = nc.scalar.activation(V[rows, :, :, HD * b:HD * b + HD],
                                                src_v[rows].rearrange("p t (h d) -> p t h d", h=HEADS), ACT.Copy)
                last.then_inc(sem["v_copied"], 1)

            def context_high(n):
                act.wait_ge(sem["ctx_loaded"], 16 * n + 16)
                if type(n) is not int or n > 0:
                    act.wait_ge(sem["v_full"], n)
                nc.scalar.activation(R(c_hi[:, :, :]), ctx_in[:, :, :], ACT.Copy).then_inc(sem["c_hi"], 1)

            def split_high(n):
                act.wait_ge(*loaded(n))
                nc.scalar.activation(R(pieces[n][1]), stage(n, pieces[n][1]), ACT.Copy).then_inc(sem["stage_hi"], 1)

            def exps(i, j):
                act.wait_ge(sem["st_full"], HEADS * i + j + 1)
                if j % 2 == 0:
                    act.wait_ge(sem["pv_done"], PAIRS * i + max(j // 2 - 1, 0))
                nc.scalar.activation(PT[:, j % 4].rearrange("p t q -> p (t q)"), work[:, BANK[("st", j)], :],
                                     ACT.Exp).then_inc(sem["exp_done"], 1)

            def relu(n, u):
                act.wait_ge(sem["hid_full"], UNITS * n + u + 1)
                if u >= 2:
                    act.wait_ge(sem["hl_done"], 2 * (UNITS * n + u - 1))
                    act.wait_ge(sem["w2_done"], UNITS * n + u - 1)
                for a in range(2):
                    k = 2 * u + a
                    for dst in (h32[:, u % 2, a, :], R(hh[:, u % 2, a, :])):
                        last = nc.scalar.activation(dst, hid[:, u % 2, a, :], ACT.Relu, bias=bias1[:, k:k + 1])
                    last.then_inc(sem["relu_done"], 1)

            def unit(i, u, ffn):
                if ffn:
                    relu(i - 1, u)
                else:
                    for n in unit_pieces(u):
                        split_high(n)

            def iteration(i, ffn, more):
                if more:
                    context_high(i + 1)
                for u in range(1, 4):
                    unit(i, u, ffn)
                high(i, "mT_full", work[:, BANK[("mT", 0)], 0:P], mT[:, 0, :], "mT_hi")
                unit(i, 4, ffn)
                if more:
                    front_x(i + 1)
                unit(i, 5, ffn)
                if more:
                    front_qk(i + 1)
                if not ffn:
                    act.wait_ge(*low_done(2 * STAGES - 1))
                    act.wait_ge(*low_done(2 * STAGES - 2))
                exps(i, 0)
                exps(i, 1)
                for p in range(PAIRS):
                    if p in PAIR_UP:
                        unit(i, PAIR_UP[p], ffn)
                    if p + 1 < PAIRS:
                        exps(i, 2 * p + 2)
                        exps(i, 2 * p + 3)
                unit(i, 9, ffn)
                high(i, "at_full", work_bank("at"), a_hi[:, :, :], "at_hi")
                unit(i, 10, ffn)
                unit(i, 11, ffn)
                act.wait_ge(sem["x2T_full"], i + 1)
                nc.scalar.activation(R(X2[:, 0, 0]), work_bank("x2T"), ACT.Copy).then_inc(sem["x2_hi"], 1)
                if more:
                    front_v(i + 1)
                relu(i, 0)

            def projection_high(n):
                w = PROJ_ORDER[n]
                act.wait_ge(sem[f"proj_loaded{n}"], 16)
                nc.scalar.activation(R(wp_hi[:, w]), PT[:, w], ACT.Copy).then_inc(sem["proj_hi"], 1)

            projection_high(0)
            context_high(0)
            projection_high(1)
            front_x(0, work[:, 2, :].rearrange("p (c t) -> p c t", c=2))
            front_qk(0, nd[:, 0], nd[:, 1])
            projection_high(2)
            projection_high(3)
            act.wait_ge(sem["zeroed"], 6)
            front_v(0, acc[:, :, :])
            for n in range(EARLY_PIECES):
                split_high(n)
            iteration(0, False, True)
            with act.Fori(1, BATCH - 1) as i:
                iteration(i, True, True)
            iteration(BATCH - 1, True, False)
            for u in range(1, UNITS):
                relu(BATCH - 1, u)

        @block.vector
        def _(dve):
            def low(i, hi_done, src, hi, dst, done, scale=1.0):
                dve.wait_ge(sem[hi_done], i + 1)
                nc.vector.scalar_tensor_tensor(out=R(dst), in0=src, scalar=scale, in1=hi, op0=ALU.mult,
                                               op1=ALU.subtract).then_inc(sem[done], 1)

            def work_bank(name):
                return work[:, BANK[(name, 0)], :].rearrange("p (c t) -> p c t", c=2)

            def norm_stats(i, src, which):
                step = f"ln{which + 1}_step"
                for t in range(TT):
                    last = nc.vector.bn_stats(stats[:, which, t, :], src[:, t, :])
                last.then_inc(sem[step], 1)
                dve.wait_ge(sem[step], 2 * i + 1)
                nc.vector.memset(pause[0:1, :], 0.0)
                for t in range(TT):
                    last = nc.vector.bn_aggr(mv[:, which, t, :], stats[:, which, t, :])
                last.then_inc(sem[step], 1)

            def norm_apply(i, src, which):
                dve.wait_ge(sem[f"rstd{which + 1}_done"], i + 1)
                for t in range(TT):
                    last = nc.vector.tensor_scalar(xhat[:, t, :], src[:, t, :], mv[:, which, t, 0:1],
                                                   rstd[:, which, t:t + 1], ALU.subtract, ALU.mult)
                last.then_inc(sem[f"ln{which + 1}_done"], 1)

            def norm1_stats(n):
                dve.wait_ge(sem["x_loaded"], 16 * n + 16)
                norm_stats(n, xin, 0)

            def norm1_apply(n):
                if type(n) is not int or n > 1:
                    dve.wait_ge(sem["x2T_full"], n - 1)
                norm_apply(n, xin, 0)

            def front_xT(n, src=None):
                low(n, "xT_hi", work_bank("xT") if src is None else src, a_hi[:, :, :], a_lo[:, :, :], "xT_lo")

            def front_qk(n, src_q=None, src_k=None):
                low(n, "k_hi", work_bank("k") if src_k is None else src_k, kn[:, 0], kn[:, 1], "k_lo")
                low(n, "q_hi", work_bank("q") if src_q is None else src_q, qn[:, 0], qn[:, 1], "q_lo", QSCALE)

            def maximum(i, j):
                dve.wait_ge(sem["s_full"], PAIRS * TT * i + j + 1)
                t, p = j // PAIRS, j % PAIRS
                nc.vector.tensor_reduce(nmax[:, t, 8 * p:8 * p + 8],
                                        work[:, BANK[("s", j)], :].rearrange("q (b k) -> q b k", k=BLOCK),
                                        AX_X, ALU.max, negate=True).then_inc(sem["max_done"], 1)

            def divide(i, p):
                dve.wait_ge(sem["pv_done"], PAIRS * i + p + 1)
                nc.vector.reciprocal(T[:, p, :], nd[:, p % 2, 1, :]).then_inc(sem["inverted"], 1)
                dve.wait_ge(sem["inverted"], PAIRS * i + p + 1)
                nc.vector.tensor_tensor(T[:, p, :], nd[:, p % 2, 0, :], T[:, p, :], ALU.mult) \
                    .then_inc(sem["t_done"], 1)

            def residual(i):
                dve.wait_ge(sem["wo_full"], i + 1)
                dve.wait_ge(sem["res_loaded"], 16 * i + 16)
                nc.vector.tensor_tensor(x1[:, :, :], work_bank("wo"), x1[:, :, :], ALU.add) \
                    .then_inc(sem["x1_done"], 1)

            def norm2_stats(i):
                dve.wait_ge(sem["x1_done"], i + 1)
                norm_stats(i, x1, 1)

            def norm2_apply(i, more):
                if more:
                    dve.wait_ge(sem["xT_full"], i + 2)
                norm_apply(i, x1, 1)

            def gate_scores(i):
                dve.wait_ge(sem["ln2_done"], i + 1)
                for e in range(2):
                    for t in range(TT):
                        last = nc.vector.tensor_tensor_reduce(
                            out=PT[:, e, t, :], in0=xhat[:, t, :], in1=gate[:, e, :], scale=1.0, scalar=0.0,
                            op0=ALU.mult, op1=ALU.add, accum_out=gsc[:, e, t:t + 1])
                last.then_inc(sem["gate_step"], 1)

            def choose(i):
                dve.wait_ge(sem["gate_step"], 2 * i + 1)
                nc.vector.tensor_tensor(mask[:, :], gsc[:, 1, :], gsc[:, 0, :], ALU.is_gt) \
                    .then_inc(sem["gate_step"], 1)
                dve.wait_ge(sem["gate_step"], 2 * i + 2)
                for t in range(TT):
                    last = nc.vector.tensor_scalar(diag[:, t, :], id16[:, :], mask[:, t:t + 1], None, ALU.mult)
                last.then_inc(sem["diag_done"], 1)

            def shared_low(i):
                low(i, "x2_hi", work_bank("x2T"), X2[:, 0, 0], X2[:, 0, 1], "x2_lo")

            def finish(n):
                dve.wait_ge(sem["w2_done"], UNITS * n + UNITS)
                dve.wait_ge(sem["x1b_done"], n + 1)
                nc.vector.tensor_tensor(x1b[:, :, :], acc[:, :, :], x1b[:, :, :], ALU.add) \
                    .then_inc(sem["y_done"], 1)

            def split_low(n):
                dve.wait_ge(sem["stage_hi"], n + 1)
                _, hi, lo = pieces[n]
                nc.vector.tensor_tensor(R(lo), stage(n, lo), hi, ALU.subtract).then_inc(sem["stage_lo_dve"], 1)

            def unit(i, u, ffn):
                if not ffn:
                    for n in unit_pieces(u):
                        if by_vector(n):
                            split_low(n)

            def iteration(i, ffn, more):
                for u in range(4):
                    for j in range(4 * u, 4 * u + 4):
                        maximum(i, j)
                    unit(i, u, ffn)
                    if more and u == 1:
                        norm1_stats(i + 1)
                if more:
                    norm1_apply(i + 1)
                low(i, "mT_hi", work[:, BANK[("mT", 0)], 0:P], mT[:, 0, :], mT[:, 1, :], "m_lo")
                if more:
                    front_xT(i + 1)
                unit(i, 4, ffn)
                if more:
                    front_qk(i + 1)
                unit(i, 5, ffn)
                for p in range(PAIRS):
                    if p in PAIR_UP:
                        unit(i, PAIR_UP[p], ffn)
                    if p == 0:
                        dve.wait_ge(sem["q_bounced"], 16 * (i + more))
                        dve.wait_ge(sem["k_bounced"], 16 * (i + more))
                    divide(i, p)
                unit(i, 9, ffn)
                low(i, "at_hi", work_bank("at"), a_hi[:, :, :], a_lo[:, :, :], "at_lo")
                unit(i, 10, ffn)
                unit(i, 11, ffn)
                residual(i)
                norm2_stats(i)
                norm2_apply(i, more)
                gate_scores(i)
                shared_low(i)
                choose(i)
                if ffn:
                    finish(i - 1)
                dve.wait_ge(sem["mk_full"], i + 1)
                nc.vector.tensor_copy(maskT[:, :], work[:, BANK[("mk", 0)], 0:SEQ]).then_inc(sem["mask_copied"], 1)

            def projection_low(n):
                w = PROJ_ORDER[n]
                dve.wait_ge(sem["proj_hi"], n + 1)
                nc.vector.tensor_tensor(R(wp_lo[:, w]), PT[:, w], wp_hi[:, w], ALU.subtract) \
                    .then_inc(sem["proj_lo"], 1)

            norm1_stats(0)
            norm1_apply(0)
            projection_low(0)
            projection_low(1)
            front_xT(0, work[:, 2, :].rearrange("p (c t) -> p c t", c=2))
            front_qk(0, nd[:, 0], nd[:, 1])
            projection_low(2)
            projection_low(3)
            dve.wait_ge(sem["indicator_loaded"], 16)
            dve.wait_ge(sem["consts_loaded"], 16 * 7)
            dve.wait_ge(sem["zeroed"], 6)
            rows = slice(SHIFT_ROW, SHIFT_ROW + SROWS)
            for s in range(2):
                nc.vector.tensor_copy(R(KP[rows, :, s, :]), x1[rows, s, None, :].to_broadcast([SROWS, PAIRS, SEQ]))
            nc.vector.tensor_copy(id16[:, :], id32[:, :])
            nc.vector.tensor_tensor(bias2[:, :], bias2[:, :], maskT[:, :], ALU.add).then_inc(sem["bias_summed"], 1)
            dve.wait_ge(sem["bias_summed"], 1)
            nc.vector.tensor_tensor(bias2[:, :], bias2[:, :], flat(mT), ALU.add) \
                .then_inc(sem["consts_made"], 1)
            for n in range(EARLY_PIECES):
                if by_vector(n):
                    split_low(n)
            iteration(0, False, True)
            with dve.Fori(1, BATCH - 1) as i:
                iteration(i, True, True)
            iteration(BATCH - 1, True, False)
            second_input(nc.vector, dve, BATCH - 1)
            first_input(nc.vector, dve, BATCH - 1)
            finish(BATCH - 1)

        @block.gpsimd
        def _(pool):
            def context_low(n):
                pool.wait_ge(sem["c_hi"], n + 1)
                nc.gpsimd.tensor_tensor(R(c_lo[:, :, :]), ctx_in[:, :, :], c_hi[:, :, :], ALU.subtract) \
                    .then_inc(sem["c_lo"], 1)

            def reciprocal_deviation(i, which):
                pool.wait_ge(sem[f"ln{which + 1}_step"], 2 * i + 2)
                nc.gpsimd.tensor_tensor(veps[:, which, :], mv[:, which, :, 1], eps[:, :], ALU.add) \
                    .then_inc(sem[f"veps{which + 1}_done"], 1)
                pool.wait_ge(sem[f"veps{which + 1}_done"], i + 1)
                nc.gpsimd.tensor_tensor(rstd[:, which, :], veps[:, which, :], power[:, :], ALU.pow) \
                    .then_inc(sem[f"rstd{which + 1}_done"], 1)

            def hidden_low(n, u):
                for a in range(2):
                    pool.wait_ge(sem["relu_done"], 2 * (UNITS * n + u) + a + 1)
                    nc.gpsimd.tensor_tensor(R(hl[:, u % 2, a]), h32[:, u % 2, a], hh[:, u % 2, a],
                                            ALU.subtract).then_inc(sem["hl_done"], 1)

            def add_bias(i):
                pool.wait_ge(sem["x1_done"], i + 1)
                pool.wait_ge(sem["ln2_done"], i + 1)
                pool.wait_ge(sem["out_done"], 16 * i)
                nc.gpsimd.tensor_tensor(x1b[:, :, :], x1[:, :, :], bias2[:, None, :].to_broadcast([P, TT, D]),
                                        ALU.add).then_inc(sem["x1b_done"], 1)

            def load(n):
                if SLOTS[n] in SLOTS[:n]:
                    last = max(m for m in range(n) if SLOTS[m] == SLOTS[n])
                    pool.wait_ge(*low_done(last))
                elif SLOTS[n] >= LATE_STAGES:
                    pool.wait_ge(sem["proj_lo"], 2 if SLOTS[n] < LATE_STAGES + 2 else 4)
                pool.dma_start(stage(n, pieces[n][0]), pieces[n][0]).then_inc(loaded(n)[0], 16)

            def split_low(n):
                pool.wait_ge(sem["stage_hi"], n + 1)
                _, hi, lo = pieces[n]
                nc.gpsimd.tensor_tensor(R(lo), stage(n, lo), hi, ALU.subtract).then_inc(sem["stage_lo_pool"], 1)

            def split_and_load(n):
                if not by_vector(n):
                    split_low(n)
                if SLOTS[n] in SLOTS[n + 1:]:
                    load(SLOTS.index(SLOTS[n], n + 1))

            def beside(n, u):
                if u == 0:
                    second_input(nc.gpsimd, pool, n)
                if u == 1:
                    first_input(nc.gpsimd, pool, n)
                if u == 3:
                    add_bias(n)

            def iteration(i, ffn, more):
                for u in range(UNITS):
                    if ffn and u == UNITS - 1:
                        reciprocal_deviation(i, 1)
                    if ffn:
                        hidden_low(i - 1, u)
                        beside(i - 1, u)
                    else:
                        for n in unit_pieces(u):
                            split_and_load(n)
                    if more and u == 2:
                        reciprocal_deviation(i + 1, 0)
                        context_low(i + 1)
                if not ffn:
                    reciprocal_deviation(i, 1)

            nc.gpsimd.memset(power[:, :], -0.5).then_inc(sem["zeroed"], 1)
            nc.gpsimd.memset(eps[:, :], EPS).then_inc(sem["zeroed"], 1)
            nc.gpsimd.memset(KP[:, :, :, :], 0.0).then_inc(sem["zeroed"], 1)
            pool.wait_ge(sem["zeroed"], 3)
            reciprocal_deviation(0, 0)
            context_low(0)
            for n in range(LATE_STAGES + 2):
                load(n)
            nc.gpsimd.memset(QP[:, :, :], 0.0).then_inc(sem["zeroed"], 1)
            nc.gpsimd.memset(V[:, :, :, :], 0.0).then_inc(sem["zeroed"], 1)
            nc.gpsimd.memset(ones16[:, :], 1.0).then_inc(sem["zeroed"], 1)
            for n in range(LATE_STAGES + 2, STAGES):
                load(n)
            for n in range(EARLY_PIECES):
                split_and_load(n)
            iteration(0, False, True)
            with pool.Fori(1, BATCH - 1) as i:
                iteration(i, True, True)
            iteration(BATCH - 1, True, False)
            for u in range(UNITS):
                hidden_low(BATCH - 1, u)
                if u == 3:
                    add_bias(BATCH - 1)


def kernel(**inputs):
    import numpy as np
    import concourse.bacc as bacc
    from concourse.bass_utils import run_bass_kernel_spmd

    def lay(a):
        return np.ascontiguousarray(a)

    def cols(w):
        w = np.asarray(w)
        return w.reshape(-1, P, w.shape[-1]).transpose(1, 0, 2)

    pattern_blocks, band = 8, 3
    seen = np.zeros((NBLK, NBLK), np.float32)
    for r in range(NBLK):
        for c in range(pattern_blocks):
            if abs(r - c) <= band:
                seen[r, min(c, NBLK - 1)] += 1
    part = np.arange(P)
    blocksum = (part[:, None] // BLOCK == np.arange(32)[None] // HD).astype(np.float32)
    same = ((part[:, None] // 64 == np.arange(32)[None] // HD)
            & (part[:, None] % HD == np.arange(32)[None] % HD))
    headsum = seen.T[part // HD % NBLK][:, :, None] * same[:, None, :]
    indicator = np.zeros((2, 2, NBLK, 2, SEQ), np.float32)
    for s in range(2):
        for b in range(NBLK):
            indicator[:, s, b, s, BLOCK * b:BLOCK * b + BLOCK] = 1.0
    w1 = [inputs["L0_ffn_sw1"], inputs["L0_ffn_w1"][0], inputs["L0_ffn_w1"][1]]
    w2 = [inputs["L0_ffn_sw2"], inputs["L0_ffn_w2"][0], inputs["L0_ffn_w2"][1]]
    b1 = [inputs["L0_ffn_sb1"], inputs["L0_ffn_b1"][0], inputs["L0_ffn_b1"][1]]
    b2 = [inputs["L0_ffn_sb2"], inputs["L0_ffn_b2"][0], inputs["L0_ffn_b2"][1]]
    arrays = {
        "x": lay(inputs["x"]),
        "ctxT": lay(np.asarray(inputs["ctx_1024"]).transpose(0, 2, 1)),
        "wT": lay(np.stack([cols(np.asarray(inputs[f"L0_xattn_W{n}"]).T) for n in "qkvo"])),
        "w1": lay(np.stack([cols(w) for w in w1], axis=1)),
        "w2": lay(np.concatenate([cols(w) for w in w2], axis=1)),
        "b1": lay(np.concatenate([np.asarray(b).reshape(-1, P).T for b in b1], axis=1)),
        "b2": lay(np.stack([np.asarray(b) for b in b2])),
        "gate_w": lay(inputs["L0_ffn_gate_w"]),
        "ident": np.eye(P, dtype=np.float32),
        "indicator": lay(indicator.reshape(SROWS, 2, SEQ)),
        "blocksum": lay(blocksum),
        "headsum": lay(headsum),
    }
    nc = bacc.Bacc("TRN2", target_bir_lowering=False, num_devices=1)
    args = [nc.dram_tensor(name, a.shape, F32, kind="ExternalInput").ap() for name, a in arrays.items()]
    out = nc.dram_tensor("out", (BATCH, SEQ, D), F32, kind="ExternalOutput").ap()
    xattn_ffn(nc, *args, out)
    r = run_bass_kernel_spmd(nc, [arrays], core_ids=[0])
    return r.results[0]["out"]
```
